# Optimizing a Trainium2 kernel written in Bass

```python
import numpy as np
import jax
import jax.numpy as jnp

def _softmax(x, axis=-1):
    return jax.nn.softmax(x, axis=axis)

def _gelu(x):
    return jax.nn.gelu(x, approximate=True)

def _silu(x):
    return jax.nn.silu(x)

def _sigmoid(x):
    return jax.nn.sigmoid(x)

def _layernorm(x, axis=-1, eps=1e-05):
    m = jnp.mean(x, axis=axis, keepdims=True)
    v = jnp.var(x, axis=axis, keepdims=True)
    return (x - m) / jnp.sqrt(v + eps)

def _scatter_add(tgt, idx, src, axis=0):
    return tgt.at[idx].add(src)

def _segment_sum(src, seg, n):
    return jax.ops.segment_sum(src, seg, n)
kernel_name = 'mk_xattn_ffn_d1_seqx_r8_05dd63'

def setup_inputs(seed: int=0):
    np.random.seed(seed)
    _w = jnp.asarray

    def _rec_inputs():
        import jax
        import jax.numpy as jnp
        _rk = jax.random.key(seed)
        x = 0.002226 + 0.9996 * jax.random.normal(jax.random.fold_in(_rk, 1), (4, 256, 128), jnp.float32)
        _lenS = 256 - jax.random.randint(jax.random.fold_in(_rk, 7), (4,), 0, max(1, 256 // 4) + 1, jnp.int32)
        _lenS2 = 256 - jax.random.randint(jax.random.fold_in(_rk, 8), (4,), 0, max(1, 256 // 4) + 1, jnp.int32)
        _ctx_1024P = jax.random.normal(jax.random.fold_in(_rk, 11), (4, 16, 128), jnp.float32)
        _ctx_1024c = jax.random.dirichlet(jax.random.fold_in(_rk, 511), 0.3 * jnp.ones((16,), jnp.float32), (4, 256))
        _ctx_1024t = jnp.einsum('bsk,bkd->bsd', _ctx_1024c, _ctx_1024P)
        _ctx_1024t = _ctx_1024t * jax.lax.rsqrt(jnp.mean(jnp.square(_ctx_1024t)) + 1e-12) * 0.953939
        ctx_1024 = -0.000125008 + 0.999885 * (_ctx_1024t + 0.3 * jax.random.normal(jax.random.fold_in(_rk, 611), (4, 256, 128), jnp.float32))
        _validS = jnp.arange(256)[None, :] < _lenS[:, None]
        _validS2 = jnp.arange(256)[None, :] < _lenS2[:, None]
        _causal = jnp.tril(jnp.ones((256, 256), dtype=bool))
        mask_BxS2_bf1 = jnp.ones((4, 256), dtype=bool)
        return (x, ctx_1024, mask_BxS2_bf1)
    x, ctx_1024, mask_BxS2_bf1 = _rec_inputs()

    def _L0_xattn_setup():
        import jax, jax.numpy as jnp
        import numpy as np
        DIM = 128
        HEADS = 16
        DIM_HEAD = 64
        INNER = HEADS * DIM_HEAD
        EPS = 1e-05

        def layer_norm(x, gamma, beta):
            mu = jnp.mean(x, axis=-1, keepdims=True)
            var = jnp.var(x, axis=-1, keepdims=True)
            return (x - mu) * jax.lax.rsqrt(var + EPS) * gamma + beta
        key = jax.random.key(seed)
        ks = jax.random.split(key, 8)
        b, n, m = (8, 512, 64)
        x = jax.random.normal(ks[0], (b, n, DIM), dtype=jnp.float32)
        latents = jax.random.normal(ks[1], (b, m, DIM), dtype=jnp.float32)
        mask = jnp.ones((b, n), dtype=bool)
        s = 0.02
        Wq = jax.random.normal(ks[2], (DIM, INNER), dtype=jnp.float32) * s
        Wkv = jax.random.normal(ks[3], (DIM, 2 * INNER), dtype=jnp.float32) * s
        Wout = jax.random.normal(ks[4], (INNER, DIM), dtype=jnp.float32) * s
        g_x = jnp.ones((DIM,), jnp.float32)
        b_x = jnp.zeros((DIM,), jnp.float32)
        g_l = jnp.ones((DIM,), jnp.float32)
        b_l = jnp.zeros((DIM,), jnp.float32)
        g_o = jnp.ones((DIM,), jnp.float32)
        b_o = jnp.zeros((DIM,), jnp.float32)
        return {'x': x, 'latents': latents, 'mask': mask, 'g_x': g_x, 'b_x': b_x, 'g_l': g_l, 'b_l': b_l, 'Wq': Wq, 'Wkv': Wkv, 'Wout': Wout, 'g_o': g_o, 'b_o': b_o}
    _L0_xattn_all = _L0_xattn_setup()
    _L0_xattn_in = {k: v for k, v in _L0_xattn_all.items() if k in ('g_x', 'b_x', 'g_l', 'b_l', 'Wq', 'Wkv', 'Wout', 'g_o', 'b_o')}
    del _L0_xattn_all

    def _L0_ffn_setup():
        import jax, jax.numpy as jnp
        import numpy as np
        TOP_K = 8
        key = jax.random.key(seed)
        ks = jax.random.split(key, 6)
        B, S, D, F, E = (2, 128, 128, 64, 64)
        x = jax.random.normal(ks[0], (B, S, D), dtype=jnp.float32)
        centroids = jax.random.normal(ks[1], (E, D), dtype=jnp.float32) * 0.05
        expert_biases = jnp.zeros((E,), dtype=jnp.float32)
        Ws_up = jax.random.normal(ks[2], (D, F), dtype=jnp.float32) / np.sqrt(D)
        Ws_down = jax.random.normal(ks[3], (F, D), dtype=jnp.float32) / np.sqrt(F)
        W_up = jax.random.normal(ks[4], (E, D, F), dtype=jnp.float32) / np.sqrt(D)
        W_down = jax.random.normal(ks[5], (E, F, D), dtype=jnp.float32) / np.sqrt(F)
        return {'x': x, 'centroids': centroids, 'expert_biases': expert_biases, 'Ws_up': Ws_up, 'Ws_down': Ws_down, 'W_up': W_up, 'W_down': W_down}
    _L0_ffn_all = _L0_ffn_setup()
    _L0_ffn_in = {k: v for k, v in _L0_ffn_all.items() if k in ('centroids', 'expert_biases', 'Ws_up', 'Ws_down', 'W_up', 'W_down')}
    del _L0_ffn_all
    return {'x': x, 'ctx_1024': ctx_1024, 'mask_BxS2_bf1': mask_BxS2_bf1, 'L0_xattn_g_x': _L0_xattn_in['g_x'], 'L0_xattn_b_x': _L0_xattn_in['b_x'], 'L0_xattn_g_l': _L0_xattn_in['g_l'], 'L0_xattn_b_l': _L0_xattn_in['b_l'], 'L0_xattn_Wq': _L0_xattn_in['Wq'], 'L0_xattn_Wkv': _L0_xattn_in['Wkv'], 'L0_xattn_Wout': _L0_xattn_in['Wout'], 'L0_xattn_g_o': _L0_xattn_in['g_o'], 'L0_xattn_b_o': _L0_xattn_in['b_o'], 'L0_ffn_centroids': _L0_ffn_in['centroids'], 'L0_ffn_expert_biases': _L0_ffn_in['expert_biases'], 'L0_ffn_Ws_up': _L0_ffn_in['Ws_up'], 'L0_ffn_Ws_down': _L0_ffn_in['Ws_down'], 'L0_ffn_W_up': _L0_ffn_in['W_up'], 'L0_ffn_W_down': _L0_ffn_in['W_down']}

def reference(x, ctx_1024, mask_BxS2_bf1, L0_xattn_g_x, L0_xattn_b_x, L0_xattn_g_l, L0_xattn_b_l, L0_xattn_Wq, L0_xattn_Wkv, L0_xattn_Wout, L0_xattn_g_o, L0_xattn_b_o, L0_ffn_centroids, L0_ffn_expert_biases, L0_ffn_Ws_up, L0_ffn_Ws_down, L0_ffn_W_up, L0_ffn_W_down):
    import jax
    import jax.numpy as jnp

    def _L0_xattn_ref(x, latents, mask, g_x, b_x, g_l, b_l, Wq, Wkv, Wout, g_o, b_o):
        import jax, jax.numpy as jnp
        import numpy as np
        DIM = 128
        HEADS = 16
        DIM_HEAD = 64
        INNER = HEADS * DIM_HEAD
        EPS = 1e-05

        def layer_norm(x, gamma, beta):
            mu = jnp.mean(x, axis=-1, keepdims=True)
            var = jnp.var(x, axis=-1, keepdims=True)
            return (x - mu) * jax.lax.rsqrt(var + EPS) * gamma + beta
        scale = DIM_HEAD ** (-0.5)
        xn = layer_norm(x, g_x, b_x)
        ln = layer_norm(latents, g_l, b_l)
        b, m = (ln.shape[0], ln.shape[1])
        q = jnp.einsum('bnd,de->bne', ln, Wq)
        kv_in = jnp.concatenate([xn, ln], axis=1)
        kv = jnp.einsum('bnd,de->bne', kv_in, Wkv)
        k, v = jnp.split(kv, 2, axis=-1)

        def split_heads(t):
            return t.reshape(t.shape[0], t.shape[1], HEADS, DIM_HEAD).transpose(0, 2, 1, 3)
        q, k, v = (split_heads(q), split_heads(k), split_heads(v))
        q = q * scale
        sim = jnp.einsum('bhid,bhjd->bhij', q, k)
        full_mask = jnp.concatenate([mask, jnp.ones((b, m), dtype=bool)], axis=1)
        max_neg = -jnp.finfo(sim.dtype).max
        sim = jnp.where(full_mask[:, None, None, :], sim, max_neg)
        attn = jax.nn.softmax(sim, axis=-1)
        out = jnp.einsum('bhij,bhjd->bhid', attn, v)
        out = out.transpose(0, 2, 1, 3).reshape(b, m, INNER)
        out = jnp.einsum('bne,ed->bnd', out, Wout)
        return layer_norm(out, g_o, b_o)

    def _L0_ffn_ref(x, centroids, expert_biases, Ws_up, Ws_down, W_up, W_down):
        import jax, jax.numpy as jnp
        import numpy as np
        TOP_K = 8
        B, S, D = x.shape
        E = centroids.shape[0]
        T = B * S
        xf = x.reshape(T, D)
        shared = jax.nn.silu(xf @ Ws_up) @ Ws_down
        aff = xf @ centroids.T
        biased = aff + expert_biases
        _, idx = jax.lax.top_k(biased, TOP_K)
        sel = jnp.take_along_axis(aff, idx, axis=1)
        w = jax.nn.sigmoid(sel)
        w = w / (jnp.sum(w, axis=-1, keepdims=True) + 1e-08)
        cw = jnp.zeros((T, E), dtype=x.dtype).at[jnp.arange(T)[:, None], idx].add(w)
        h = jax.nn.silu(jnp.einsum('td,edf->etf', xf, W_up))
        y = jnp.einsum('etf,efd->etd', h, W_down)
        routed = jnp.einsum('etd,te->td', y, cw)
        return (shared + routed).reshape(B, S, D)
    x = x + _L0_xattn_ref(ctx_1024, _layernorm(x, axis=-1), mask_BxS2_bf1, L0_xattn_g_x, L0_xattn_b_x, L0_xattn_g_l, L0_xattn_b_l, L0_xattn_Wq, L0_xattn_Wkv, L0_xattn_Wout, L0_xattn_g_o, L0_xattn_b_o)
    x = x + _L0_ffn_ref(_layernorm(x, axis=-1), L0_ffn_centroids, L0_ffn_expert_biases, L0_ffn_Ws_up, L0_ffn_Ws_down, L0_ffn_W_up, L0_ffn_W_down)
    return x

_drawn_inputs = setup_inputs


def setup_inputs(seed=0):
    import zlib

    import numpy as np

    out = dict(_drawn_inputs(seed))
    spreads = {'L0_xattn_g_x': (1.0, 0.2),
     'L0_xattn_b_x': (0.0, 0.1),
     'L0_xattn_g_l': (1.0, 0.568),
     'L0_xattn_b_l': (0.0, 0.1),
     'L0_xattn_g_o': (1.0, 0.2),
     'L0_xattn_b_o': (0.0, 0.1),
     'L0_ffn_expert_biases': (0.0, 0.1)}
    factors = {}
    for name, (base, spread) in spreads.items():
        noise = np.random.default_rng([zlib.crc32(name.encode()), seed]).standard_normal(out[name].shape)
        drawn = base * np.exp(spread * noise) if base else spread * noise
        out[name] = jnp.asarray(drawn.astype(out[name].dtype))
    for name, factor in factors.items():
        out[name] = (out[name] * factor).astype(out[name].dtype)
    return out
```

```python
from contextlib import ExitStack

import concourse.bass as bass
from concourse import mybir

F32 = mybir.dt.float32
F32R = mybir.dt.float32r
F16 = mybir.dt.float16
U8 = mybir.dt.uint8
ALU = mybir.AluOpType
ACT = mybir.ActivationFunctionType
AX_X = mybir.AxisListType.X

P = 128
EPS = 1e-5
COMBINE_EPS = 1e-8
TOP_K = 8
MASKED = -1e30
LEAST = -3.0e38
RANGE16 = 4096.0


def xattn_moe(nc, x, ctx_in, mask, g_x, b_x, g_l, b_l, wq, wkv, wout, g_o, b_o,
              centroids, expert_biases, ws_up, ws_down, w_up, w_down, out):
    B, S, D = x.shape
    T = B * S
    NT = T // P
    KEYS = 2 * S
    KT = KEYS // P
    QT = S // P
    DH = 64
    INNER = wq.shape[1]
    PAIRS = INNER // (2 * DH)
    SCALE = DH ** -0.5
    E, _, FF = w_up.shape
    FT = E * FF // P
    TILES = 2 * QT
    assert D == P and TILES == 4 and KEYS == 512

    stack = ExitStack()
    with stack:
        def sem(name):
            return stack.enter_context(nc.semaphore(name))

        def lay(offset, specs):
            made = []
            for name, shape, dt in specs:
                size = 4 if dt in (F32, F32R) else 2 if dt == F16 else 1
                for n in shape[1:]:
                    size *= n
                made.append(nc.alloc_sbuf_tensor_at(name, shape, dt, offset=offset))
                offset += (size + 31) // 32 * 32
            return made, offset

        base = (nc.sbuf_base + 31) // 32 * 32
        (ident, one16, ident16, zeros16, cols, stats, mv, rs, tmp, neg_max, p_sum, p_scaled, p_rinv,
         ), top = lay(base, [
            ("ident", [P, P], F32), ("one16", [P, P], F16), ("ident16", [P, P], F16), ("zeros16", [P, 512], F16),
            ("cols", [P, 4], F32), ("stats", [P, 2 * NT, 6], F32), ("mv", [P, 2 * NT, 2], F32),
            ("rs", [P, 2 * NT], F32), ("tmp", [P, 2, 2 * NT], F32),
            ("neg_max", [P, TILES], F32), ("p_sum", [P, TILES], F32), ("p_scaled", [P, TILES], F32), ("p_rinv", [P, TILES], F32),
        ])
        late_base = top
        (w_all, kv_hi, kv_lo, q_hi, q_lo), top = lay(top, [
            ("w_all", [P, PAIRS, 6, P], F32R),
            ("kv_hi", [P, B, KEYS], F32R), ("kv_lo", [P, B, KEYS], F32R),
            ("q_hi", [P, 2, T], F32R), ("q_lo", [P, 2, T], F32R),
        ])
        late_end = top
        (m_st, wo_st, v_st, mask_add), top = lay(top, [
            ("m_st", [P, 4, P], F32R), ("wo_st", [P, 2, P], F32R),
            ("v_st", [P, B, KT, P], F32), ("mask_add", [P, B, KEYS], F32),
        ])
        v_base = top
        (v_all,), top = lay(top, [("v_all", [P, B * KT, INNER], F32)])
        v_end = top
        step_base = top
        (tok, x_in, kvT, wqT, wkT), end1 = lay(step_base, [
            ("tok", [P, B, KT, P], F32), ("x_in", [P, NT, P], F32), ("kvT", [P, B, KEYS], F32),
            ("wqT", [P, PAIRS, P], F32), ("wkT", [P, PAIRS, 2, P], F32),
        ])
        (sc, prob, p_hi, p_lo, probT, ao_hi, ao_lo), end2 = lay(step_base, [
            ("sc", [P, 2, KEYS], F32), ("prob", [P, TILES, KEYS], F32),
            ("p_hi", [P, TILES, KEYS], F16), ("p_lo", [P, TILES, KEYS], F16),
            ("probT", [P, 2, KT, S], F32), ("ao_hi", [P, S], F32R), ("ao_lo", [P, S], F32R),
        ])
        top = max(end1, end2)
        raw_base = top
        (wq_s, wkv_s, wv_hi, wv_lo, wo_s, mask_u8), end1 = lay(raw_base, [
            ("wq_s", [P, INNER], F32), ("wkv_s", [P, 2 * INNER], F32),
            ("wv_hi", [P, INNER], F32R), ("wv_lo", [P, INNER], F32R),
            ("wo_s", [P, PAIRS, P], F32), ("mask_u8", [P, B, S], U8),
        ])
        (wup_s, wdn_s), end2 = lay(raw_base, [
            ("wup_s", [P, E, FF], F32), ("wdn_s", [P, FT, P], F32),
        ])
        assert max(end1, end2) <= nc.sbuf_usable_end, (max(end1, end2), nc.sbuf_usable_end)
        (sel16, x_res, go_row, bo_row, bias_row, cent, centT, wsu, wsd, wsu_hi, wsu_lo, wsd_hi, wsd_lo,
         outT, x1, xh, xfT, xf_hi, xf_lo, aff, biased, left, gate, combine, w_sum, top8, cw16, cwT16),\
            end = lay(v_base, [
                ("sel16", [P, E, FF], F16), ("x_res", [P, NT, P], F32), ("go_row", [P, P], F32),
                ("bo_row", [P, P], F32), ("bias_row", [P, E], F32), ("cent", [E, P], F32),
                ("centT", [P, E], F32), ("wsu", [P, FF], F32), ("wsd", [FF, P], F32),
                ("wsu_hi", [P, FF], F32R), ("wsu_lo", [P, FF], F32R),
                ("wsd_hi", [FF, P], F32R), ("wsd_lo", [FF, P], F32R),
                ("outT", [P, T], F32), ("x1", [P, NT, P], F32), ("xh", [P, NT, P], F32),
                ("xfT", [P, T], F32), ("xf_hi", [P, T], F32R), ("xf_lo", [P, T], F32R),
                ("aff", [P, NT, E], F32), ("biased", [P, NT, E], F32), ("left", [P, NT, E], F32),
                ("gate", [P, NT, E], F32), ("combine", [P, NT, E], F32), ("w_sum", [P, 2, NT], F32),
                ("top8", [P, NT, 8], F32), ("cw16", [P, NT, 2, E], F16), ("cwT16", [P, T], F16),
            ])
        assert end <= v_end
        (h, h_hi, h_lo, wu_hi, wu_lo, wd_hi, wd_lo, yT, y_out), end = lay(late_base, [
            ("h", [P, 2, T], F32), ("h_hi", [P, 2, T], F32R), ("h_lo", [P, 2, T], F32R),
            ("wu_hi", [P, 2, P], F32R), ("wu_lo", [P, 2, P], F32R),
            ("wd_hi", [P, 2, P], F32R), ("wd_lo", [P, 2, P], F32R),
            ("yT", [P, T], F32), ("y_out", [P, NT, P], F32),
        ])
        assert end <= late_end

        ps = stack.enter_context(nc.psum_tensor("ps", [P, 8, 512], F32))
        OUT_BANK, SCORE_BANK, T_BANK, AV_BANK, Q_BANK = 0, 2, 4, 6, 7
        U_BANK, CW_BANK, Y_BANK = 2, 6, 0

        s_x, s_ctx, s_cols, s_mask = sem("s_x"), sem("s_ctx"), sem("s_cols"), sem("s_mask")
        s_wq, s_wkv, s_wo = sem("s_wq"), sem("s_wkv"), sem("s_wo")
        s_late = sem("s_late")
        s_wup, s_wdn = sem("s_wup"), sem("s_wdn")
        s_mst, s_wst = sem("s_mst"), sem("s_wst")
        s_vst = [sem(f"s_vst{b}") for b in range(B)]
        s_pool = sem("s_pool")
        s_dve = sem("s_dve")
        s_var, s_std = sem("s_var"), sem("s_std")
        s_tok = sem("s_tok")
        s_tp = sem("s_tp")
        s_wT = sem("s_wT")
        s_kvT, s_kvhi, s_kvlo = sem("s_kvT"), sem("s_kvhi"), sem("s_kvlo")
        s_m, s_mhi, s_mlo = sem("s_m"), sem("s_mhi"), sem("s_mlo")
        s_wvhi, s_wvlo = sem("s_wvhi"), sem("s_wvlo")
        s_wohi, s_wolo = sem("s_wohi"), sem("s_wolo")
        s_v, s_vact, s_vdve = sem("s_v"), sem("s_vact"), sem("s_vdve")
        s_maskadd = sem("s_maskadd")
        s_held = sem("s_held")
        s_score, s_masked, s_exp = sem("s_score"), sem("s_masked"), sem("s_exp")
        s_scaled, s_rinv = sem("s_scaled"), sem("s_rinv")
        s_phi, s_plo, s_pT, s_pTsb = sem("s_phi"), sem("s_plo"), sem("s_pT"), sem("s_pTsb")
        s_av, s_aohi, s_aolo, s_wout = sem("s_av"), sem("s_aohi"), sem("s_aolo"), sem("s_wout")
        s_q, s_qhi, s_qlo = sem("s_q"), sem("s_qhi"), sem("s_qlo")
        s_outT, s_outTt, s_d2 = sem("s_outT"), sem("s_outTt"), sem("s_d2")
        s_var2, s_std2 = sem("s_var2"), sem("s_std2")
        s_xh, s_xhT, s_xfT, s_xfhi, s_xflo = (sem("s_xh"), sem("s_xhT"), sem("s_xfT"), sem("s_xfhi"),
                                              sem("s_xflo"))
        s_cent, s_centT, s_aff, s_affsb, s_eneg = (sem("s_cent"), sem("s_centT"), sem("s_aff"),
                                                   sem("s_affsb"), sem("s_eneg"))
        s_xres = sem("s_xres")
        s_cw, s_cwt, s_cwT, s_sel = sem("s_cw"), sem("s_cwt"), sem("s_cwT"), sem("s_sel")
        s_sw, s_su, s_ssilu, s_shi, s_slo, s_sd = (sem("s_sw"), sem("s_su"), sem("s_ssilu"),
                                                   sem("s_shi"), sem("s_slo"), sem("s_sd"))
        s_wu, s_wd, s_pchain = sem("s_wu"), sem("s_wd"), sem("s_pchain")
        s_u, s_cwb, s_silu, s_h, s_hhi, s_hlo, s_down = (sem("s_u"), sem("s_cwb"), sem("s_silu"),
                                                         sem("s_h"), sem("s_hhi"), sem("s_hlo"),
                                                         sem("s_down"))
        s_yT, s_yt, s_y, s_out = sem("s_yT"), sem("s_yt"), sem("s_y"), sem("s_out")

        def row(v):
            return v.rearrange("(a d) -> a d", a=1)

        def col(v):
            return v.rearrange("(d a) -> d a", a=1)

        block = stack.enter_context(nc.Block())

        @block.sync
        def _(sp):
            sp.dma_start(x_in[:, :, :], x.rearrange("b (q p) d -> p (b q) d", p=P)).then_inc(s_x, 16)
            for b in range(B):
                sp.dma_start(tok[:, b, 0:QT, :],
                             ctx_in[b, :, :].rearrange("(q p) d -> p q d", p=P)).then_inc(s_ctx, 16)
            for i, v in enumerate((g_x, b_x, g_l, b_l)):
                sp.dma_start(cols[:, i:i + 1], col(v)).then_inc(s_cols, 16)
            sp.dma_start(mask_u8[:, :, :],
                         mask.rearrange("(o b) s -> o b s", o=1).broadcast_to([P, B, S])).then_inc(s_mask, 16)

            def stage_m(pair):
                sp.dma_start(m_st[:, :, :].bitcast(F32), w_all[:, bass.ds(pair, 1), 0:4, :]
                             .rearrange("p a k c -> p (a k) c").bitcast(F32)).then_inc(s_mst, 16)

            def stage_wo(pair):
                sp.dma_start(wo_st[:, :, :].bitcast(F32), w_all[:, bass.ds(pair, 1), 4:6, :]
                             .rearrange("p a k c -> p (a k) c").bitcast(F32)).then_inc(s_wst, 16)

            def stage_v(pair, b):
                sp.dma_start(v_st[:, b, :, :], v_all[:, b * KT:(b + 1) * KT, bass.ds(pair * P, P)])\
                    .then_inc(s_vst[b], 16)

            sp.wait_ge(s_mlo, PAIRS // 2)
            stage_m(0)
            sp.wait_ge(s_wolo, 1)
            stage_wo(0)
            for b in range(B):
                sp.wait_ge(s_vact, (b + 1) * KT)
                sp.wait_ge(s_vdve, (b + 1) * KT)
                stage_v(0, b)
            with sp.Fori(0, PAIRS - 1) as pr:
                sp.wait_ge(s_q, (pr + 1) * 4)
                stage_m(pr + 1)
                for b in range(B):
                    sp.wait_ge(s_av, pr * B + (b + 2))
                    stage_v(pr + 1, b)
                sp.wait_ge(s_wout, pr * B + (B + 1))
                stage_wo(pr + 1)
            for b in range(B):
                sp.wait_ge(s_vst[b], 16 * PAIRS)
            sp.dma_start(x_res[:, :, :], x.rearrange("b (q p) d -> p (b q) d", p=P)).then_inc(s_late, 16)
            sp.dma_start(go_row[:, :], row(g_o).broadcast_to([P, P])).then_inc(s_late, 16)
            sp.dma_start(bo_row[:, :], row(b_o).broadcast_to([P, P])).then_inc(s_late, 16)
            sp.dma_start(bias_row[:, :], row(expert_biases).broadcast_to([P, E])).then_inc(s_late, 16)
            sp.dma_start(cent[:, :], centroids).then_inc(s_late, 16)
            sp.dma_start(wsu[:, :], ws_up).then_inc(s_late, 16)
            sp.dma_start(wsd[:, :], ws_down).then_inc(s_late, 16)
            for half in range(2):
                sp.wait_ge(s_y, half + 1)
                sp.dma_start(out.rearrange("b (q p) d -> p (b q) d", p=P)[:, 4 * half:4 * half + 4, :],
                             y_out[:, 4 * half:4 * half + 4, :]).then_inc(s_out, 16)
            sp.wait_ge(s_out, 32)

        LATE = 16 * 7

        @block.gpsimd
        def _(pool):
            pool.memset(ident[:, :], 0.0).then_inc(s_pool, 1)
            pool.memset(one16[:, :], 0.0).then_inc(s_pool, 1)
            pool.memset(ident16[:, :], 0.0).then_inc(s_pool, 1)
            pool.memset(zeros16[:, :], 0.0).then_inc(s_pool, 1)
            pool.memset(wkT[:, :, :, :], 0.0).then_inc(s_pool, 1)
            pool.wait_ge(s_pool, 3)
            for m, fill in ((ident, 1.0), (one16, 1.0), (ident16, 1.0 / RANGE16)):
                pool.affine_select(out=m[:, :], in_=m[:, :], compare_op=ALU.not_equal, fill=fill,
                                   base=0, pattern=[[-1, P]], channel_multiplier=1).then_inc(s_pool, 1)

            def split_high(pr, step_in_pair, t, guard=True):
                if t % 2 == 0:
                    pool.wait_ge(s_rinv, pr * (2 * B) + (step_in_pair * 2 + t // 2 + 1))
                if guard:
                    pool.wait_ge(s_pT, pr * (B * TILES) + ((step_in_pair - 1) * TILES + t + 1))
                pool.tensor_tensor(p_hi[:, t, :], prob[:, t, :],
                                   p_rinv[:, t:t + 1].broadcast_to([P, KEYS]), ALU.mult).then_inc(s_phi, 1)

            for t in range(TILES):
                split_high(0, 0, t, guard=False)
            with pool.Fori(0, PAIRS - 1) as pr:
                for b in range(B):
                    for t in range(TILES):
                        split_high(pr, b + 1, t)
            for b in range(B - 1):
                for t in range(TILES):
                    split_high(PAIRS - 1, b + 1, t)

            pool.wait_ge(s_late, LATE)
            pool.tensor_tensor(x_res[:, :, :], x_res[:, :, :],
                               bo_row[:, :].unsqueeze(1).broadcast_to([P, NT, P]), ALU.add).then_inc(s_xres, 1)

            for b in range(B):
                pool.wait_ge(s_vst[b], 16 * PAIRS)
            pool.memset(sel16[:, :, :], 0.0).then_inc(s_sel, 1)
            pool.wait_ge(s_sel, 1)
            for part in range(2):
                pool.affine_select(out=sel16[:, :, :], in_=sel16[:, :, :], compare_op=ALU.not_equal,
                                   fill=1.0 / RANGE16, base=-part * E, pattern=[[-1, E], [0, FF]],
                                   channel_multiplier=1).then_inc(s_sel, 1)
                pool.wait_ge(s_sel, part + 2)

            pool.wait_ge(s_wup, 32)
            pool.wait_ge(s_wdn, 32)
            pool.wait_ge(s_wout, PAIRS * B + 1)

            up_cols = wup_s[:, :, :].rearrange("p e f -> p (e f)")
            down_cols = wdn_s[:, :, :].rearrange("p t d -> p (t d)")

            def split(w, hi, lo, f, n, done):
                pool.tensor_copy(hi, w[:, bass.ds(f * P, P)]).then_inc(s_pchain, 1)
                pool.wait_ge(s_pchain, n + 1)
                pool.sem_inc(s_held, 1)
                pool.tensor_tensor(lo, w[:, bass.ds(f * P, P)], hi.bitcast(F32), ALU.subtract)\
                    .then_inc(done, 1)

            def split_up(f, u, n, guard=True):
                if guard:
                    pool.wait_ge(s_u, f - 1)
                split(up_cols, wu_hi[:, u, :], wu_lo[:, u, :], f, n, s_wu)

            def split_down(f, u, n, guard=True):
                if guard:
                    pool.wait_ge(s_down, f - 1)
                split(down_cols, wd_hi[:, u, :], wd_lo[:, u, :], f, n, s_wd)

            split_up(0, 0, 0, guard=False)
            split_up(1, 1, 1, guard=False)
            split_up(2, 0, 2)
            split_down(0, 0, 3, guard=False)
            split_up(3, 1, 4)
            split_down(1, 1, 5, guard=False)
            with pool.Fori(1, FT // 2 - 1) as i:
                split_up(i * 2 + 2, 0, i * 4 + 2)
                split_down(i * 2, 0, i * 4 + 3)
                split_up(i * 2 + 3, 1, i * 4 + 4)
                split_down(i * 2 + 1, 1, i * 4 + 5)
            split_down(FT - 2, 0, 2 * FT - 2)
            split_down(FT - 1, 1, 2 * FT - 1)

        @block.scalar
        def _(act):
            act.dma_start(wkv_s[:, :], wkv).then_inc(s_wkv, 16)
            act.dma_start(wq_s[:, :], wq).then_inc(s_wq, 16)
            act.dma_start(wo_s[:, :, :], wout.rearrange("(r p) d -> p r d", p=P)).then_inc(s_wo, 16)

            for n in range(2):
                act.wait_ge(s_var, n + 1)
                width = (2 * NT, NT)[n]
                act.activation(rs[:, 0:width], tmp[:, 0, 0:width], ACT.Sqrt).then_inc(s_std, 1)
            act.wait_ge(s_wkv, 16)
            act.activation(wv_hi[:, :], wkv_s[:, INNER:2 * INNER], ACT.Copy).then_inc(s_wvhi, 1)
            act.wait_ge(s_wo, 16)
            act.activation(w_all[:, :, 4, :], wo_s[:, :, :], ACT.Copy).then_inc(s_wohi, 1)
            for g in range(PAIRS // 2):
                act.wait_ge(s_m, g + 1)
                act.activation(w_all[:, 2 * g:2 * g + 2, 0:2, :],
                               ps[:, SCORE_BANK + g, :].rearrange("p (r k c) -> p r k c", r=2, k=2),
                               ACT.Copy).then_inc(s_mhi, 1)
            act.wait_ge(s_cols, 64)
            for b in range(B):
                act.wait_ge(s_tp, 5 + b)
                for part in range(2):
                    act.activation(kvT[:, b, part * S:(part + 1) * S],
                                   ps[:, AV_BANK + b % 2, part * S:(part + 1) * S], ACT.Identity,
                                   bias=cols[:, 2 * part + 1:2 * part + 2],
                                   scale=cols[:, 2 * part:2 * part + 1]).then_inc(s_kvT, 1)

            def exp(k, t, guard=True):
                act.wait_ge(s_masked, k + 1)
                if guard:
                    act.wait_ge(s_plo, k - (TILES - 1))
                act.activation(prob[:, t, :], sc[:, t % 2, :], ACT.Exp, bias=neg_max[:, t:t + 1],
                               scale=-1.0, accum_out=p_sum[:, t:t + 1]).then_inc(s_exp, 1)

            def evac_t(k, step, t):
                act.wait_ge(s_pT, k + 1)
                if t == 0:
                    act.wait_ge(s_av, step + 1)
                head, qt = t // QT, t % QT
                act.activation(probT[:, head, :, qt * P:(qt + 1) * P],
                               ps[:, T_BANK + t % 2, :].rearrange("p (k c) -> p k c", k=KT),
                               ACT.Copy).then_inc(s_pTsb, 1)

            def ao_high(step):
                act.wait_ge(s_av, step + 2)
                act.wait_ge(s_wout, step + 1)
                act.activation(ao_hi[:, :], ps[:, AV_BANK, 0:S], ACT.Copy).then_inc(s_aohi, 1)

            def q_high(c, quarter):
                act.wait_ge(s_q, c + 1)
                head, half = quarter % 2, quarter // 2
                act.activation(q_hi[:, head, half * 512:(half + 1) * 512], ps[:, Q_BANK, :],
                               ACT.Copy).then_inc(s_qhi, 1)

            for c in range(4):
                q_high(c, c)
            for t in range(TILES):
                exp(t, t, guard=False)
            for n in range(0, 2 * B * KT, 2):
                act.wait_ge(s_v, n + 1)
                act.activation(v_all[:, n // 2, 0:512], ps[:, T_BANK + n % 4, :], ACT.Copy)\
                    .then_inc(s_vact, 1)

            def pair_body(pr, last):
                for b in range(B):
                    step = pr * B + b
                    k = pr * (B * TILES) + b * TILES
                    more = not (last and b == B - 1)
                    evac_t(k, step, 0)
                    for t in range(1, TILES):
                        evac_t(k + t, step, t)
                        if more:
                            exp(k + (TILES + t - 1), t - 1)
                    if more:
                        exp(k + (2 * TILES - 1), TILES - 1)
                    if not last:
                        q_high(pr * 4 + (4 + b), b)
                    ao_high(step)

            act.wait_ge(s_vdve, B * KT)
            act.wait_ge(s_wolo, 1)
            for cut in range(2):
                half = slice(cut * E // 2, (cut + 1) * E // 2)
                act.dma_start(wup_s[:, half, :], w_up[half, :, :].rearrange("e d f -> d e f")).then_inc(s_wup, 16)
            for cut in range(2):
                half = slice(cut * E // 2, (cut + 1) * E // 2)
                act.dma_start(wdn_s[:, cut * FT // 2:(cut + 1) * FT // 2, :],
                              w_down[half, :, :].rearrange("(t two) f d -> (two f) t d", two=2))\
                   .then_inc(s_wdn, 16)

            act.sem_inc(s_pTsb, 2)
            with act.Fori(0, PAIRS - 1) as pr:
                pair_body(pr, False)
            pair_body(PAIRS - 1, True)

            act.wait_ge(s_wout, PAIRS * B + 1)
            act.activation(outT[:, 512:1024], ps[:, OUT_BANK + 1, :], ACT.Copy).then_inc(s_outT, 1)
            for n in range(2):
                act.wait_ge(s_var2, n + 1)
                act.activation(rs[:, 0:NT], tmp[:, 0, 0:NT], ACT.Sqrt).then_inc(s_std2, 1)
            for half in range(2):
                act.wait_ge(s_xhT, half + 1)
                act.activation(xfT[:, half * 512:(half + 1) * 512], ps[:, 4 + half, :], ACT.Copy)\
                    .then_inc(s_xfT, 1)
            for half in range(2):
                act.wait_ge(s_xfT, half + 1)
                act.activation(xf_hi[:, half * 512:(half + 1) * 512], xfT[:, half * 512:(half + 1) * 512],
                               ACT.Copy).then_inc(s_xfhi, 1)
            act.wait_ge(s_affsb, 1)
            act.activation(gate[:, :, :], aff[:, :, :], ACT.Exp, scale=-1.0).then_inc(s_eneg, 1)
            act.wait_ge(s_su, 1)
            act.activation(h[0:FF, 0, :].rearrange("p (a c) -> p a c", a=2), ps[0:FF, U_BANK:U_BANK + 2, :],
                           ACT.Silu).then_inc(s_ssilu, 1)
            act.wait_ge(s_ssilu, 1)
            act.activation(h_hi[0:FF, 0, :], h[0:FF, 0, :], ACT.Copy).then_inc(s_shi, 1)

            def silu(f, u, guard=True):
                act.wait_ge(s_u, f + 1)
                if guard:
                    act.wait_ge(s_hlo, f - 1)
                act.activation(h[:, u, :].rearrange("p (a c) -> p a c", a=2),
                               ps[:, U_BANK + 2 * u:U_BANK + 2 * u + 2, :], ACT.Silu).then_inc(s_silu, 1)

            def h_high(f, u, guard=True):
                act.wait_ge(s_h, f + 1)
                if guard:
                    act.wait_ge(s_down, f - 1)
                act.activation(h_hi[:, u, :], h[:, u, :], ACT.Copy).then_inc(s_hhi, 1)

            act.wait_ge(s_sd, 1)
            silu(0, 0, guard=False)
            silu(1, 1, guard=False)
            h_high(0, 0, guard=False)
            silu(2, 0)
            h_high(1, 1, guard=False)
            with act.Fori(0, FT // 2 - 2) as i:
                silu(i * 2 + 3, 1)
                h_high(i * 2 + 2, 0)
                silu(i * 2 + 4, 0)
                h_high(i * 2 + 3, 1)
            silu(FT - 1, 1)
            h_high(FT - 2, 0)
            h_high(FT - 1, 1)
            act.wait_ge(s_down, FT)
            act.activation(yT[:, 512:1024], ps[:, Y_BANK + 1, :], ACT.Copy).then_inc(s_yT, 1)

        @block.tensor
        def _(pe):
            def three(o, a_hi, a_lo, b_hi, b_lo, start=True, stop=True):
                skip = not (start and stop)
                pe.matmul(o, a_hi, b_hi, start=start, stop=False, skip_group_check=skip)
                pe.matmul(o, a_hi, b_lo, start=False, stop=False, skip_group_check=skip)
                return pe.matmul(o, a_lo, b_hi, start=False, stop=stop, skip_group_check=skip)

            pe.wait_ge(s_pool, 8)
            for g, (w, loaded) in enumerate(((wkv_s, s_wkv), (wkv_s, s_wkv), (wq_s, s_wq), (wq_s, s_wq))):
                pe.wait_ge(loaded, 16)
                for j in range(4):
                    r = 4 * (g % 2) + j
                    mm = pe.transpose(ps[:, SCORE_BANK + g, j * P:(j + 1) * P], w[:, r * P:(r + 1) * P],
                                      ident[:, :])
                mm.then_inc(s_tp, 1)
            pe.wait_ge(s_wT, 6)
            for g in range(PAIRS // 2):
                for j in range(2):
                    r = 2 * g + j
                    mm = pe.matmul(ps[:, SCORE_BANK + g, j * 256:(j + 1) * 256], wqT[:, r, :],
                                   wkT[:, r, :, :], start=True, stop=True)
                mm.then_inc(s_m, 1)
            for b in range(B):
                pe.wait_ge(s_tok, b + 1)
                if b >= 2:
                    pe.wait_ge(s_kvT, 2 * (b - 1))
                for j in range(KT):
                    mm = pe.transpose(ps[:, AV_BANK + b % 2, j * P:(j + 1) * P], tok[:, b, j, :],
                                      ident[:, :])
                mm.then_inc(s_tp, 1)
            for n in range(2):
                mm = pe.matmul(ps[:, OUT_BANK + n, :], zeros16[:, 0:P], zeros16[:, :], start=True, stop=True)
            mm.then_inc(s_wout, 1)

            def queries(c, quarter):
                head, half = quarter % 2, quarter // 2
                rows = slice(2 * half, 2 * half + 2)
                three(ps[:, Q_BANK, :].rearrange("p (b s) -> p b s", b=2),
                      m_st[:, head, :], m_st[:, 2 + head, :],
                      kv_hi[:, rows, S:2 * S], kv_lo[:, rows, S:2 * S]).then_inc(s_q, 1)

            def scores(b, t):
                head, qt = t // QT, t % QT
                at = b * S + qt * P
                three(ps[:, SCORE_BANK + t % 2, :], q_hi[:, head, at:at + P], q_lo[:, head, at:at + P],
                      kv_hi[:, b, :], kv_lo[:, b, :]).then_inc(s_score, 1)

            pe.wait_ge(s_kvlo, B)
            pe.wait_ge(s_mst, 16)
            for c in range(4):
                if c:
                    pe.wait_ge(s_qlo, c)
                queries(c, c)
            pe.wait_ge(s_qlo, 4)
            pe.wait_ge(s_mlo, PAIRS // 2)
            for t in range(TILES):
                if t >= 2:
                    pe.wait_ge(s_masked, t - 1)
                scores(0, t)
            pe.wait_ge(s_wvlo, 1)
            for n in range(2 * B * KT):
                if n >= 4:
                    pe.wait_ge(s_vdve if n % 2 else s_vact, n // 2 - 1)
                b, j, half = n // (2 * KT), n // 2 % KT, n % 2
                cut = slice(half * 512, (half + 1) * 512)
                three(ps[:, T_BANK + n % 4, :], kv_hi[:, b, j * P:(j + 1) * P], kv_lo[:, b, j * P:(j + 1) * P],
                      wv_hi[:, cut], wv_lo[:, cut]).then_inc(s_v, 1)
            pe.wait_ge(s_vact, B * KT)
            pe.wait_ge(s_vdve, B * KT)
            pe.sem_inc(s_av, 1)

            def transpose_p(k, t):
                pe.wait_ge(s_plo, k + 1)
                pe.wait_ge(s_pTsb, k + 1)
                for j in range(KT):
                    cut = slice(j * P, (j + 1) * P)
                    o = ps[:, T_BANK + t % 2, cut]
                    pe.matmul(o, p_hi[:, t, cut], ident16[:, :], start=True, stop=False)
                    mm = pe.matmul(o, p_lo[:, t, cut], ident16[:, :], start=False, stop=True)
                mm.then_inc(s_pT, 1)

            def attend(pr, step, b):
                pe.wait_ge(s_pTsb, step * TILES + (TILES + 2))
                pe.wait_ge(s_vst[b], pr * 16 + 16)
                pe.wait_ge(s_aolo, step + 1)
                for j in range(KT):
                    for head in range(2):
                        cut = slice(head * DH, (head + 1) * DH)
                        mm = pe.matmul(ps[cut, AV_BANK, 0:S], v_st[:, b, j, cut], probT[:, head, j, :],
                                       start=(j == 0), stop=(j == KT - 1), skip_group_check=True)
                mm.then_inc(s_av, 1)

            def project(step, b):
                pe.wait_ge(s_aolo, step + 2)
                at = b * S
                three(ps[:, OUT_BANK + at // 512, at % 512:at % 512 + S], wo_st[:, 0, :], wo_st[:, 1, :],
                      ao_hi[:, :], ao_lo[:, :], start=False, stop=False).then_inc(s_wout, 1)

            def pair_body(pr, first, last):
                for b in range(B):
                    step = pr * B + b
                    k = pr * (B * TILES) + b * TILES
                    more = not (last and b == B - 1)
                    for t in range(TILES):
                        transpose_p(k + t, t)
                        if t == 1 and not (first and b == 0):
                            if b == 1:
                                pe.wait_ge(s_wst, pr * 16 + 16)
                            project(step - 1, (b - 1) % B)
                        if more:
                            pe.wait_ge(s_masked, k + (TILES + t - 1))
                            if t == 0 and b == B - 1:
                                pe.wait_ge(s_qlo, pr * 4 + 6)
                            if t == 0 and b == 1:
                                pe.wait_ge(s_qlo, pr * 4 + 4)
                            scores((b + 1) % B, t)
                    if not last:
                        pe.wait_ge(s_mst, pr * 16 + 32)
                        pe.wait_ge(s_qlo, pr * 4 + (4 + b))
                        queries(pr * 4 + (4 + b), b)
                    attend(pr, step, b)

            pair_body(0, True, False)
            with pe.Fori(1, PAIRS - 1) as pr:
                pair_body(pr, False, False)
            pair_body(PAIRS - 1, False, True)
            project(PAIRS * B - 1, B - 1)

            for g in range(2):
                pe.wait_ge(s_outT, 2)
                for j in range(4):
                    mm = pe.transpose(ps[:, 2 + g, j * P:(j + 1) * P],
                                      outT[:, (4 * g + j) * P:(4 * g + j + 1) * P], ident[:, :])
                mm.then_inc(s_outTt, 1)
            pe.wait_ge(s_late, LATE)
            pe.transpose(ps[:, 6, 0:E], cent[:, :], ident[0:E, 0:E]).then_inc(s_cent, 1)
            pe.wait_ge(s_xh, 1)
            for g in range(2):
                for j in range(4):
                    mm = pe.transpose(ps[:, 4 + g, j * P:(j + 1) * P], xh[:, 4 * g + j, :], ident[:, :])
                mm.then_inc(s_xhT, 1)
            pe.wait_ge(s_centT, 1)
            pe.wait_ge(s_xfT, 2)
            for j in range(NT):
                mm = pe.matmul(ps[:, 7, j * E:(j + 1) * E], xfT[:, j * P:(j + 1) * P], centT[:, :],
                               start=True, stop=True)
            mm.then_inc(s_aff, 1)
            pe.wait_ge(s_xflo, 2)
            pe.wait_ge(s_sw, 4)
            for half in range(2):
                cut = slice(half * 512, (half + 1) * 512)
                mm = three(ps[0:FF, U_BANK + half, :], wsu_hi[:, :], wsu_lo[:, :], xf_hi[:, cut], xf_lo[:, cut])
            mm.then_inc(s_su, 1)

            def up(f, u):
                pe.wait_ge(s_wu, f + 1)
                for half in range(2):
                    cut = slice(half * 512, (half + 1) * 512)
                    mm = three(ps[:, U_BANK + 2 * u + half, :], wu_hi[:, u, :], wu_lo[:, u, :],
                               xf_hi[:, cut], xf_lo[:, cut])
                mm.then_inc(s_u, 1)

            def spread(f, guard=True):
                if guard:
                    pe.wait_ge(s_h, f)
                w = sel16[:, :, :].rearrange("p e f -> p (e f)")[:, bass.ds(f * P, P)]
                for half in range(2):
                    mm = pe.matmul(ps[:, CW_BANK + half, :], w, cwT16[:, half * 512:(half + 1) * 512],
                                   start=True, stop=True)
                mm.then_inc(s_cwb, 1)

            def down(f, u):
                pe.wait_ge(s_hlo, f + 1)
                pe.wait_ge(s_wd, f + 1)
                for half in range(2):
                    cut = slice(half * 512, (half + 1) * 512)
                    mm = three(ps[:, Y_BANK + half, :], wd_hi[:, u, :], wd_lo[:, u, :],
                               h_hi[:, u, cut], h_lo[:, u, cut], start=False, stop=False)
                mm.then_inc(s_down, 1)

            pe.wait_ge(s_slo, 1)
            for half in range(2):
                cut = slice(half * 512, (half + 1) * 512)
                o = ps[:, Y_BANK + half, :]
                pe.matmul(o, wsd_hi[:, :], h_hi[0:FF, 0, cut], start=True, stop=False, skip_group_check=True)
                pe.matmul(o, wsd_hi[:, :], h_lo[0:FF, 0, cut], start=False, stop=False, skip_group_check=True)
                mm = pe.matmul(o, wsd_lo[:, :], h_hi[0:FF, 0, cut], start=False, stop=False,
                               skip_group_check=True)
            mm.then_inc(s_sd, 1)
            up(0, 0)
            up(1, 1)
            pe.wait_ge(s_cw, 1)
            pe.wait_ge(s_affsb, 1)
            t16 = ps[:, CW_BANK, :].bitcast(F16)
            for j in range(NT):
                mm = pe.transpose(t16[:, j * P:(j + 1) * P], cw16[:, j, :, :].rearrange("p a e -> p (a e)"), one16[:, :])
            mm.then_inc(s_cwt, 1)
            pe.wait_ge(s_sel, 3)
            pe.wait_ge(s_cwT, 1)
            spread(0, guard=False)
            spread(1)

            def slot(f, u):
                pe.wait_ge(s_silu, f + 1)
                up(f + 2, u)
                spread(f + 2)
                down(f, u)

            with pe.Fori(0, FT // 2 - 1) as i:
                slot(i * 2, 0)
                slot(i * 2 + 1, 1)
            down(FT - 2, 0)
            down(FT - 1, 1)
            pe.wait_ge(s_yT, 2)
            for g in range(2):
                for j in range(4):
                    mm = pe.transpose(ps[:, 2 + g, j * P:(j + 1) * P],
                                      yT[:, (4 * g + j) * P:(4 * g + j + 1) * P], ident[:, :])
                mm.then_inc(s_yt, 1)


        @block.vector
        def _(dve):
            count = [0]

            def chain(ins):
                ins.then_inc(s_dve, 1)
                count[0] += 1

            def chained():
                dve.wait_ge(s_dve, count[0])

            chain(dve.memset(mask_add[:, :, S:KEYS], 0.0))
            dve.wait_ge(s_mask, 16)
            dve.tensor_scalar(mask_add[:, :, 0:S], mask_u8[:, :, :], -MASKED, MASKED, ALU.mult, ALU.add)\
               .then_inc(s_maskadd, 1)

            def inverse_std(w, done):
                dve.wait_ge(*done)
                chain(dve.reciprocal(rs[:, 0:w], rs[:, 0:w]))
                chained()
                chain(dve.tensor_tensor(tmp[:, 1, 0:w], rs[:, 0:w], rs[:, 0:w], ALU.mult))
                chained()
                chain(dve.tensor_tensor(tmp[:, 1, 0:w], tmp[:, 1, 0:w], tmp[:, 0, 0:w], ALU.mult))
                chained()
                chain(dve.tensor_scalar(tmp[:, 1, 0:w], tmp[:, 1, 0:w], -0.5, 1.5, ALU.mult, ALU.add))
                chained()
                chain(dve.tensor_tensor(rs[:, 0:w], rs[:, 0:w], tmp[:, 1, 0:w], ALU.mult))
                chained()

            def moments(tiles):
                for j, tile in enumerate(tiles):
                    chain(dve.bn_stats(stats[:, j, :], tile))
                chained()
                for j in range(len(tiles)):
                    chain(dve.bn_aggr(mv[:, j, :], stats[:, j, :]))
                chained()

            def normalise(o, tile, j):
                return dve.tensor_scalar(o, tile, mv[:, j, 0:1], rs[:, j:j + 1], ALU.subtract, ALU.mult)

            latents = [tok[:, b, QT + q, :] for b in range(B) for q in range(QT)]
            contexts = [tok[:, b, q, :] for b in range(B) for q in range(QT)]
            raw = [x_in[:, j, :] for j in range(NT)]
            dve.wait_ge(s_x, 16)
            dve.wait_ge(s_ctx, 16 * B)
            moments(raw + contexts)
            dve.tensor_scalar(tmp[:, 0, :], mv[:, :, 1], EPS, None, ALU.add).then_inc(s_var, 1)
            dve.wait_ge(s_pool, 5)
            for g in range(2):
                dve.wait_ge(s_tp, g + 1)
                for head in range(2):
                    cut = slice(head * DH, (head + 1) * DH)
                    dve.tensor_copy(wkT[cut, 4 * g:4 * g + 4, head, :],
                                    ps[cut, SCORE_BANK + g, :].rearrange("p (r c) -> p r c", r=4))\
                       .then_inc(s_wT, 1)
            for g in range(2):
                dve.wait_ge(s_tp, g + 3)
                dve.tensor_copy(wqT[:, 4 * g:4 * g + 4, :],
                                ps[:, SCORE_BANK + 2 + g, :].rearrange("p (r c) -> p r c", r=4))\
                   .then_inc(s_wT, 1)
            inverse_std(2 * NT, (s_std, 1))
            for j in range(NT):
                chain(normalise(latents[j], raw[j], j))
            for j in range(NT):
                chain(normalise(contexts[j], contexts[j], NT + j))
            chained()
            moments(latents)
            dve.tensor_scalar(tmp[:, 0, 0:NT], mv[:, 0:NT, 1], EPS, None, ALU.add).then_inc(s_var, 1)
            inverse_std(NT, (s_std, 2))
            for b in range(B):
                chain(normalise(latents[2 * b], latents[2 * b], 2 * b))
                normalise(latents[2 * b + 1], latents[2 * b + 1], 2 * b + 1).then_inc(s_tok, 1)
            for g in range(PAIRS // 2):
                dve.wait_ge(s_mhi, g + 1)
                dve.tensor_tensor(w_all[:, 2 * g:2 * g + 2, 2:4, :],
                                  ps[:, SCORE_BANK + g, :].rearrange("p (r k c) -> p r k c", r=2, k=2),
                                  w_all[:, 2 * g:2 * g + 2, 0:2, :].bitcast(F32), ALU.subtract)\
                   .then_inc(s_mlo, 1)
            for b in range(B):
                dve.wait_ge(s_kvT, 2 * (b + 1))
                dve.tensor_copy(kv_hi[:, b, :], kvT[:, b, :]).then_inc(s_kvhi, 1)
                dve.wait_ge(s_kvhi, b + 1)
                dve.tensor_tensor(kv_lo[:, b, :], kvT[:, b, :], kv_hi[:, b, :].bitcast(F32), ALU.subtract)\
                   .then_inc(s_kvlo, 1)

            def mask_scores(k, t, guard=True):
                dve.wait_ge(s_score, k + 1)
                if guard:
                    dve.wait_ge(s_exp, k - 1)
                dve.sem_inc(s_held, 1)
                return dve.tensor_tensor_reduce(sc[:, t % 2, :], ps[:, SCORE_BANK + t % 2, :],
                                                mask_now, -SCALE, -LEAST, ALU.add, ALU.min,
                                                neg_max[:, t:t + 1]).then_inc(s_masked, 1)

            def invert(kk, t):
                dve.wait_ge(s_exp, kk * 2 + 2)
                dve.tensor_scalar(p_scaled[:, t:t + 2], p_sum[:, t:t + 2], 1.0 / RANGE16, None, ALU.mult)\
                   .then_inc(s_scaled, 1)
                dve.wait_ge(s_scaled, kk + 1)
                dve.reciprocal(p_rinv[:, t:t + 2], p_scaled[:, t:t + 2]).then_inc(s_rinv, 1)

            def split_low(k, t):
                dve.wait_ge(s_phi, k + 1)
                dve.scalar_tensor_tensor(out=p_lo[:, t, :], in0=prob[:, t, :], scalar=p_rinv[:, t:t + 1],
                                         in1=p_hi[:, t, :], op0=ALU.mult, op1=ALU.subtract)\
                   .then_inc(s_plo, 1)

            def ao_low(step):
                dve.wait_ge(s_aohi, step + 1)
                dve.tensor_tensor(ao_lo[:, :], ps[:, AV_BANK, 0:S], ao_hi[:, :].bitcast(F32),
                                  ALU.subtract).then_inc(s_aolo, 1)

            def q_low(c, quarter):
                dve.wait_ge(s_qhi, c + 1)
                head, half = quarter % 2, quarter // 2
                cut = slice(half * 512, (half + 1) * 512)
                dve.tensor_tensor(q_lo[:, head, cut], ps[:, Q_BANK, :], q_hi[:, head, cut].bitcast(F32),
                                  ALU.subtract).then_inc(s_qlo, 1)

            for c in range(4):
                q_low(c, c)
            dve.wait_ge(s_maskadd, 1)
            chained()
            mask_now = mask_add[:, 0, :]
            for t in range(TILES):
                mask_scores(t, t, guard=t >= 2)
                if t % 2:
                    invert(t // 2, t - 1)
            dve.wait_ge(s_wvhi, 1)
            dve.tensor_tensor(wv_lo[:, :], wkv_s[:, INNER:2 * INNER], wv_hi[:, :].bitcast(F32),
                              ALU.subtract).then_inc(s_wvlo, 1)
            dve.wait_ge(s_wohi, 1)
            dve.tensor_tensor(w_all[:, :, 5, :], wo_s[:, :, :], w_all[:, :, 4, :].bitcast(F32),
                              ALU.subtract).then_inc(s_wolo, 1)
            for t in range(2):
                split_low(t, t)
            for n in range(1, 2 * B * KT, 2):
                dve.wait_ge(s_v, n + 1)
                dve.tensor_copy(v_all[:, n // 2, 512:1024], ps[:, T_BANK + n % 4, :]).then_inc(s_vdve, 1)

            def pair_body(pr, last):
                nonlocal mask_now
                for b in range(B):
                    step = pr * B + b
                    k = pr * (B * TILES) + (b + 1) * TILES
                    kk = pr * (B * 2) + (b + 1) * 2
                    more = not (last and b == B - 1)
                    mask_now = mask_add[:, (b + 1) % B, :]
                    for t in range(2):
                        if more:
                            mask_scores(k + t, t)
                        split_low(k - (2 - t), t + 2)
                    if more:
                        mask_scores(k + 2, 2)
                        invert(kk, 0)
                        mask_scores(k + 3, 3)
                        split_low(k, 0)
                        invert(kk + 1, 2)
                        split_low(k + 1, 1)
                    if not last:
                        q_low(pr * 4 + (4 + b), b)
                    ao_low(step)

            dve.sem_inc(s_aolo, 1)
            with dve.Fori(0, PAIRS - 1) as pr:
                pair_body(pr, False)
            pair_body(PAIRS - 1, True)

            dve.wait_ge(s_wout, PAIRS * B + 1)
            dve.tensor_copy(outT[:, 0:512], ps[:, OUT_BANK, :]).then_inc(s_outT, 1)
            dve.wait_ge(s_late, LATE)
            dve.tensor_copy(wsu_hi[:, :], wsu[:, :]).then_inc(s_sw, 1)
            dve.tensor_copy(wsd_hi[:, :], wsd[:, :]).then_inc(s_sw, 1)
            dve.wait_ge(s_sw, 2)
            dve.tensor_tensor(wsu_lo[:, :], wsu[:, :], wsu_hi[:, :].bitcast(F32), ALU.subtract).then_inc(s_sw, 1)
            dve.tensor_tensor(wsd_lo[:, :], wsd[:, :], wsd_hi[:, :].bitcast(F32), ALU.subtract).then_inc(s_sw, 1)
            turned = [ps[:, 2 + j // 4, j % 4 * P:(j % 4 + 1) * P] for j in range(NT)]
            dve.wait_ge(s_outTt, 2)
            moments(turned)
            dve.tensor_scalar(tmp[:, 0, 0:NT], mv[:, 0:NT, 1], EPS, None, ALU.add).then_inc(s_var2, 1)
            inverse_std(NT, (s_std2, 1))
            for j in range(NT):
                chain(dve.scalar_tensor_tensor(out=x1[:, j, :], in0=turned[j], scalar=mv[:, j, 0:1],
                                               in1=go_row[:, :], op0=ALU.subtract, op1=ALU.mult))
            dve.wait_ge(s_xres, 1)
            chained()
            for j in range(NT):
                chain(dve.scalar_tensor_tensor(out=x1[:, j, :], in0=x1[:, j, :], scalar=rs[:, j:j + 1],
                                               in1=x_res[:, j, :], op0=ALU.mult, op1=ALU.add))
            chained()
            moments([x1[:, j, :] for j in range(NT)])
            dve.tensor_scalar(tmp[:, 0, 0:NT], mv[:, 0:NT, 1], EPS, None, ALU.add).then_inc(s_var2, 1)
            inverse_std(NT, (s_std2, 2))
            for j in range(NT):
                ins = normalise(xh[:, j, :], x1[:, j, :], j)
                if j < NT - 1:
                    chain(ins)
            ins.then_inc(s_xh, 1)
            dve.wait_ge(s_cent, 1)
            dve.tensor_copy(centT[:, :], ps[:, 6, 0:E]).then_inc(s_centT, 1)
            for half in range(2):
                cut = slice(half * 512, (half + 1) * 512)
                dve.wait_ge(s_xfhi, half + 1)
                dve.tensor_tensor(xf_lo[:, cut], xfT[:, cut], xf_hi[:, cut].bitcast(F32), ALU.subtract)\
                   .then_inc(s_xflo, 1)
            dve.wait_ge(s_aff, 1)
            dve.tensor_copy(aff[:, :, :], ps[:, 7, :].rearrange("p (j e) -> p j e", j=NT)).then_inc(s_affsb, 1)
            dve.wait_ge(s_affsb, 1)
            chain(dve.tensor_tensor(biased[:, :, :], aff[:, :, :],
                                    bias_row[:, :].unsqueeze(1).broadcast_to([P, NT, E]), ALU.add))
            chained()
            for j in range(NT):
                chain(dve.max(top8[:, j, :], biased[:, j, :]))
            chained()
            for j in range(NT):
                chain(dve.match_replace(left[:, j, :], top8[:, j, :], biased[:, j, :], LEAST))
            chained()
            chain(dve.tensor_tensor(biased[:, :, :], left[:, :, :], biased[:, :, :], ALU.not_equal))
            dve.wait_ge(s_eneg, 1)
            chain(dve.tensor_scalar(gate[:, :, :], gate[:, :, :], 1.0, None, ALU.add))
            chained()
            chain(dve.reciprocal(gate[:, :, :], gate[:, :, :]))
            chained()
            chain(dve.tensor_tensor(gate[:, :, :], gate[:, :, :], biased[:, :, :], ALU.mult))
            chained()
            chain(dve.tensor_reduce(w_sum[:, 0, :], gate[:, :, :], AX_X, ALU.add))
            chained()
            chain(dve.tensor_scalar(w_sum[:, 0, :], w_sum[:, 0, :], COMBINE_EPS, 1.0 / RANGE16, ALU.add, ALU.mult))
            chained()
            chain(dve.reciprocal(w_sum[:, 1, :], w_sum[:, 0, :]))
            chained()
            chain(dve.tensor_tensor(combine[:, :, :], gate[:, :, :],
                                    w_sum[:, 1, :].unsqueeze(2).broadcast_to([P, NT, E]), ALU.mult))
            chained()
            chain(dve.tensor_copy(cw16[:, :, 0, :], combine[:, :, :]))
            chained()
            dve.tensor_tensor(cw16[:, :, 1, :], combine[:, :, :], cw16[:, :, 0, :], ALU.subtract)\
               .then_inc(s_cw, 1)
            dve.wait_ge(s_shi, 1)
            dve.tensor_tensor(h_lo[0:FF, 0, :], h[0:FF, 0, :], h_hi[0:FF, 0, :].bitcast(F32), ALU.subtract)\
               .then_inc(s_slo, 1)
            dve.wait_ge(s_cwt, 1)
            dve.tensor_copy(cwT16[:, :], ps[:, CW_BANK, :].bitcast(F16)).then_inc(s_cwT, 1)

            def weigh(f, u):
                dve.wait_ge(s_silu, f + 1)
                dve.wait_ge(s_cwb, f + 1)
                hv = h[:, u, :].rearrange("p (a c) -> p a c", a=2)
                dve.tensor_tensor(hv, hv, ps[:, CW_BANK:CW_BANK + 2, :], ALU.mult).then_inc(s_h, 1)

            def h_low(f, u):
                dve.wait_ge(s_hhi, f + 1)
                dve.tensor_tensor(h_lo[:, u, :], h[:, u, :], h_hi[:, u, :].bitcast(F32), ALU.subtract)\
                   .then_inc(s_hlo, 1)

            weigh(0, 0)
            weigh(1, 1)
            h_low(0, 0)
            with dve.Fori(0, FT // 2 - 1) as i:
                weigh(i * 2 + 2, 0)
                h_low(i * 2 + 1, 1)
                weigh(i * 2 + 3, 1)
                h_low(i * 2 + 2, 0)
            h_low(FT - 1, 1)
            dve.wait_ge(s_down, FT)
            dve.tensor_copy(yT[:, 0:512], ps[:, Y_BANK, :]).then_inc(s_yT, 1)
            for half in range(2):
                dve.wait_ge(s_yt, half + 1)
                dve.tensor_tensor(y_out[:, 4 * half:4 * half + 4, :],
                                  ps[:, 2 + half, :].rearrange("p (j d) -> p j d", j=4),
                                  x1[:, 4 * half:4 * half + 4, :], ALU.add).then_inc(s_y, 1)


INPUTS = ["x", "ctx_1024", "mask_BxS2_bf1", "L0_xattn_g_x", "L0_xattn_b_x", "L0_xattn_g_l", "L0_xattn_b_l",
          "L0_xattn_Wq", "L0_xattn_Wkv", "L0_xattn_Wout", "L0_xattn_g_o", "L0_xattn_b_o",
          "L0_ffn_centroids", "L0_ffn_expert_biases", "L0_ffn_Ws_up", "L0_ffn_Ws_down", "L0_ffn_W_up",
          "L0_ffn_W_down"]


def kernel(**inputs):
    import numpy as np
    import concourse.bacc as bacc
    from concourse.bass_utils import run_bass_kernel_spmd

    nc = bacc.Bacc("TRN2", target_bir_lowering=False, num_devices=1)
    arrays, args = {}, []
    for name in INPUTS:
        a = np.ascontiguousarray(inputs[name])
        if a.dtype == np.bool_:
            a = a.view(np.uint8)
        arrays["in_" + name] = a
        args.append(nc.dram_tensor("in_" + name, a.shape, mybir.dt.from_np(a.dtype), kind="ExternalInput").ap())
    shape = inputs["x"].shape
    args.append(nc.dram_tensor("out_0", shape, F32, kind="ExternalOutput").ap())
    xattn_moe(nc, *args)
    r = run_bass_kernel_spmd(nc, [arrays], core_ids=[0])
    return r.results[0]["out_0"]
```

```python
from contextlib import ExitStack

import concourse.bass as bass
from concourse import mybir

F32 = mybir.dt.float32
F32R = mybir.dt.float32r
F16 = mybir.dt.float16
U8 = mybir.dt.uint8
ALU = mybir.AluOpType
ACT = mybir.ActivationFunctionType
AX_X = mybir.AxisListType.X

P = 128
EPS = 1e-5
COMBINE_EPS = 1e-8
TOP_K = 8
MASKED = -1e30
LEAST = -3.0e38
RANGE16 = 4096.0


def xattn_moe(nc, x, ctx_in, mask, g_x, b_x, g_l, b_l, wq, wkv, wout, g_o, b_o,
              centroids, expert_biases, ws_up, ws_down, w_up, w_down, out):
    B, S, D = x.shape
    T = B * S
    NT = T // P
    KEYS = 2 * S
    KT = KEYS // P
    QT = S // P
    DH = 64
    INNER = wq.shape[1]
    PAIRS = INNER // (2 * DH)
    SCALE = DH ** -0.5
    E, _, FF = w_up.shape
    FT = E * FF // P
    TILES = 2 * QT
    assert D == P and TILES == 4 and KEYS == 512

    stack = ExitStack()
    with stack:
        def sem(name):
            return stack.enter_context(nc.semaphore(name))

        def lay(offset, specs):
            made = []
            for name, shape, dt in specs:
                size = 4 if dt in (F32, F32R) else 2 if dt == F16 else 1
                for n in shape[1:]:
                    size *= n
                made.append(nc.alloc_sbuf_tensor_at(name, shape, dt, offset=offset))
                offset += (size + 31) // 32 * 32
            return made, offset

        base = (nc.sbuf_base + 31) // 32 * 32
        (ident, one16, ident16, zeros16, cols, stats, mv, rs, shift, tmp, neg_max, p_sum, p_scaled, p_rinv,
         ), top = lay(base, [
            ("ident", [P, P], F32), ("one16", [P, P], F16), ("ident16", [P, P], F16), ("zeros16", [P, 512], F16),
            ("cols", [P, 4], F32), ("stats", [P, 2 * NT, 6], F32), ("mv", [P, 2 * NT, 2], F32),
            ("rs", [P, 2 * NT], F32), ("shift", [P, 2 * NT], F32), ("tmp", [P, 2, 2 * NT], F32),
            ("neg_max", [P, TILES], F32), ("p_sum", [P, TILES], F32), ("p_scaled", [P, TILES], F32), ("p_rinv", [P, TILES], F32),
        ])
        late_base = top
        (w_all, kv_hi, kv_lo, q_hi, q_lo), top = lay(top, [
            ("w_all", [P, PAIRS, 6, P], F32R),
            ("kv_hi", [P, B, KEYS], F32R), ("kv_lo", [P, B, KEYS], F32R),
            ("q_hi", [P, 2, T], F32R), ("q_lo", [P, 2, T], F32R),
        ])
        late_end = top
        (m_st, wo_st, v_st, mask_add), top = lay(top, [
            ("m_st", [P, 4, P], F32R), ("wo_st", [P, 2, P], F32R),
            ("v_st", [P, B, KT, P], F32), ("mask_add", [P, B, KEYS], F32),
        ])
        v_base = top
        (v_all,), top = lay(top, [("v_all", [P, B * KT, INNER], F32)])
        v_end = top
        step_base = top
        (tok, x_in, kvT, wqT, wkT), end1 = lay(step_base, [
            ("tok", [P, B, KT, P], F32), ("x_in", [P, NT, P], F32), ("kvT", [P, B, KEYS], F32),
            ("wqT", [P, PAIRS, P], F32), ("wkT", [P, PAIRS, 2, P], F32),
        ])
        (sc, prob, p_hi, p_lo, probT, ao_hi, ao_lo), end2 = lay(step_base, [
            ("sc", [P, 2, KEYS], F32), ("prob", [P, TILES, KEYS], F32),
            ("p_hi", [P, TILES, KEYS], F16), ("p_lo", [P, TILES, KEYS], F16),
            ("probT", [P, 2, KT, S], F32), ("ao_hi", [P, S], F32R), ("ao_lo", [P, S], F32R),
        ])
        top = max(end1, end2)
        raw_base = top
        (wq_s, wkv_s, wv_hi, wv_lo, wo_s, mask_u8), end1 = lay(raw_base, [
            ("wq_s", [P, INNER], F32), ("wkv_s", [P, 2 * INNER], F32),
            ("wv_hi", [P, INNER], F32R), ("wv_lo", [P, INNER], F32R),
            ("wo_s", [P, PAIRS, P], F32), ("mask_u8", [P, B, S], U8),
        ])
        (wup_s, wdn_s), end2 = lay(raw_base, [
            ("wup_s", [P, E, FF], F32), ("wdn_s", [P, FT, P], F32),
        ])
        assert max(end1, end2) <= nc.sbuf_usable_end, (max(end1, end2), nc.sbuf_usable_end)
        (sel16, x_res, go_row, bo_row, bias_row, cent, centT, wsu, wsd, wsu_hi, wsu_lo, wsd_hi, wsd_lo,
         outT, x1, xh, xfT, xf_hi, xf_lo, aff, biased, left, gate, combine, w_sum, top8, cw16, cwT16),\
            end = lay(v_base, [
                ("sel16", [P, E, FF], F16), ("x_res", [P, NT, P], F32), ("go_row", [P, P], F32),
                ("bo_row", [P, P], F32), ("bias_row", [P, E], F32), ("cent", [E, P], F32),
                ("centT", [P, E], F32), ("wsu", [P, FF], F32), ("wsd", [FF, P], F32),
                ("wsu_hi", [P, FF], F32R), ("wsu_lo", [P, FF], F32R),
                ("wsd_hi", [FF, P], F32R), ("wsd_lo", [FF, P], F32R),
                ("outT", [P, T], F32), ("x1", [P, NT, P], F32), ("xh", [P, NT, P], F32),
                ("xfT", [P, T], F32), ("xf_hi", [P, T], F32R), ("xf_lo", [P, T], F32R),
                ("aff", [P, NT, E], F32), ("biased", [P, NT, E], F32), ("left", [P, NT, E], F32),
                ("gate", [P, NT, E], F32), ("combine", [P, NT, E], F32), ("w_sum", [P, 2, NT], F32),
                ("top8", [P, NT, 8], F32), ("cw16", [P, NT, 2, E], F16), ("cwT16", [P, T], F16),
            ])
        assert end <= v_end
        (h, h_hi, h_lo, wu_hi, wu_lo, wd_hi, wd_lo, yT, y_out), end = lay(late_base, [
            ("h", [P, 2, T], F32), ("h_hi", [P, 2, T], F32R), ("h_lo", [P, 2, T], F32R),
            ("wu_hi", [P, 2, P], F32R), ("wu_lo", [P, 2, P], F32R),
            ("wd_hi", [P, 2, P], F32R), ("wd_lo", [P, 2, P], F32R),
            ("yT", [P, T], F32), ("y_out", [P, NT, P], F32),
        ])
        assert end <= late_end

        ps = stack.enter_context(nc.psum_tensor("ps", [P, 8, 512], F32))
        OUT_BANK, SCORE_BANK, T_BANK, AV_BANK, Q_BANK = 0, 2, 4, 6, 7
        U_BANK, CW_BANK, Y_BANK = 2, 6, 0
        V_BANKS = (0, 1, 6, 7)

        CHUNKS = 2 * B * KT
        between = {7: ["q0"], 8: ["q1"], 9: ["q2"], 10: ["q3"], 13: ["s0"], 14: ["s1", "x0"], 16: ["x1"],
                   17: ["s2", "i0"], 18: ["s3", "x2"], 20: ["x3"], 21: ["lo0"], 22: ["i2"], 23: ["lo1"],
                   26: ["lo2"]}
        OPENING = [item for n in range(CHUNKS) for item in [f"v{n}"] + between.get(n, [])]
        OPENING = [(item.rstrip("0123456789"), int(item.lstrip("vqsxilo"))) for item in OPENING]

        s_x = [sem("s_x0"), sem("s_x1")]
        s_ctx = [sem("s_ctx0"), sem("s_ctx1")]
        s_cols, s_mask = sem("s_cols"), sem("s_mask")
        s_wq, s_wk, s_wv, s_wo = sem("s_wq"), sem("s_wk"), sem("s_wv"), sem("s_wo")
        s_late = sem("s_late")
        s_wup, s_wdn = sem("s_wup"), sem("s_wdn")
        s_mst, s_wst = sem("s_mst"), sem("s_wst")
        s_vst = [sem(f"s_vst{b}") for b in range(B)]
        s_pool = sem("s_pool")
        s_dve = sem("s_dve")
        s_var, s_std = sem("s_var"), sem("s_std")
        s_tok, s_tokc = sem("s_tok"), sem("s_tokc")
        s_shift = sem("s_shift")
        s_tp, s_kvtp = sem("s_tp"), sem("s_kvtp")
        s_wT = sem("s_wT")
        s_kvT, s_kvhi, s_kvlo = sem("s_kvT"), sem("s_kvhi"), sem("s_kvlo")
        s_m, s_mhi, s_mlo = sem("s_m"), sem("s_mhi"), sem("s_mlo")
        s_wvhi, s_wvlo = sem("s_wvhi"), sem("s_wvlo")
        s_wohi, s_wolo = sem("s_wohi"), sem("s_wolo")
        s_v, s_vact, s_vdve = sem("s_v"), sem("s_vact"), sem("s_vdve")
        s_maskadd = sem("s_maskadd")
        s_held = sem("s_held")
        s_score, s_masked, s_exp = sem("s_score"), sem("s_masked"), sem("s_exp")
        s_scaled, s_rinv = sem("s_scaled"), sem("s_rinv")
        s_phi, s_plo, s_pT, s_pTsb = sem("s_phi"), sem("s_plo"), sem("s_pT"), sem("s_pTsb")
        s_av, s_aohi, s_aolo, s_wout = sem("s_av"), sem("s_aohi"), sem("s_aolo"), sem("s_wout")
        s_q, s_qhi, s_qlo = sem("s_q"), sem("s_qhi"), sem("s_qlo")
        s_outT, s_outTt, s_d2 = sem("s_outT"), sem("s_outTt"), sem("s_d2")
        s_var2, s_std2 = sem("s_var2"), sem("s_std2")
        s_xh, s_xhT, s_xfT, s_xfhi, s_xflo = (sem("s_xh"), sem("s_xhT"), sem("s_xfT"), sem("s_xfhi"),
                                              sem("s_xflo"))
        s_cent, s_centT, s_aff, s_affsb, s_eneg = (sem("s_cent"), sem("s_centT"), sem("s_aff"),
                                                   sem("s_affsb"), sem("s_eneg"))
        s_xres = sem("s_xres")
        s_cw, s_cwt, s_cwT, s_sel = sem("s_cw"), sem("s_cwt"), sem("s_cwT"), sem("s_sel")
        s_sw, s_su, s_ssilu, s_shi, s_slo, s_sd = (sem("s_sw"), sem("s_su"), sem("s_ssilu"),
                                                   sem("s_shi"), sem("s_slo"), sem("s_sd"))
        s_wu, s_wd, s_pchain = sem("s_wu"), sem("s_wd"), sem("s_pchain")
        s_u, s_cwb, s_silu, s_h, s_hhi, s_hlo, s_down = (sem("s_u"), sem("s_cwb"), sem("s_silu"),
                                                         sem("s_h"), sem("s_hhi"), sem("s_hlo"),
                                                         sem("s_down"))
        s_yT, s_yt, s_y, s_out = sem("s_yT"), sem("s_yt"), sem("s_y"), sem("s_out")

        def row(v):
            return v.rearrange("(a d) -> a d", a=1)

        def col(v):
            return v.rearrange("(d a) -> d a", a=1)

        block = stack.enter_context(nc.Block())

        @block.sync
        def _(sp):
            def load_tokens(half):
                for b in (2 * half, 2 * half + 1):
                    sp.dma_start(x_in[:, QT * b:QT * (b + 1), :],
                                 x[b, :, :].rearrange("(q p) d -> p q d", p=P)).then_inc(s_x[half], 16)
                for b in (2 * half, 2 * half + 1):
                    sp.dma_start(tok[:, b, 0:QT, :],
                                 ctx_in[b, :, :].rearrange("(q p) d -> p q d", p=P)).then_inc(s_ctx[half], 16)

            load_tokens(0)
            load_tokens(1)
            for i, v in enumerate((g_x, b_x, g_l, b_l)):
                sp.dma_start(cols[:, i:i + 1], col(v)).then_inc(s_cols, 16)
            sp.dma_start(mask_u8[:, :, :],
                         mask.rearrange("(o b) s -> o b s", o=1).broadcast_to([P, B, S])).then_inc(s_mask, 16)

            def stage_m(pair):
                sp.dma_start(m_st[:, :, :].bitcast(F32), w_all[:, bass.ds(pair, 1), 0:4, :]
                             .rearrange("p a k c -> p (a k) c").bitcast(F32)).then_inc(s_mst, 16)

            def stage_wo(pair):
                sp.dma_start(wo_st[:, :, :].bitcast(F32), w_all[:, bass.ds(pair, 1), 4:6, :]
                             .rearrange("p a k c -> p (a k) c").bitcast(F32)).then_inc(s_wst, 16)

            def stage_v(pair, b):
                sp.dma_start(v_st[:, b, :, :], v_all[:, b * KT:(b + 1) * KT, bass.ds(pair * P, P)])\
                    .then_inc(s_vst[b], 16)

            sp.wait_ge(s_mlo, 1)
            stage_m(0)
            for b in range(B):
                sp.wait_ge(s_vact, (b + 1) * KT)
                sp.wait_ge(s_vdve, (b + 1) * KT)
                stage_v(0, b)
            sp.wait_ge(s_wolo, 1)
            stage_wo(0)

            def load_experts(part):
                sp.dma_start(wup_s[:, bass.ds(part * (E // PAIRS), E // PAIRS), :],
                             w_up[bass.ds(part * (E // PAIRS), E // PAIRS), :, :].rearrange("e d f -> d e f"))\
                    .then_inc(s_wup, 16)
                sp.dma_start(wdn_s[:, bass.ds(part * (FT // PAIRS), FT // PAIRS), :],
                             w_down[bass.ds(part * (E // PAIRS), E // PAIRS), :, :]
                             .rearrange("(t two) f d -> (two f) t d", two=2)).then_inc(s_wdn, 16)

            load_experts(0)
            with sp.Fori(0, PAIRS - 1) as pr:
                sp.wait_ge(s_q, (pr + 1) * 4)
                stage_m(pr + 1)
                for b in range(B):
                    sp.wait_ge(s_av, pr * B + (b + 2))
                    stage_v(pr + 1, b)
                load_experts(pr + 1)
                sp.wait_ge(s_wout, pr * B + (B + 1))
                stage_wo(pr + 1)
            for b in range(B):
                sp.wait_ge(s_vst[b], 16 * PAIRS)
            sp.dma_start(x_res[:, :, :], x.rearrange("b (q p) d -> p (b q) d", p=P)).then_inc(s_late, 16)
            sp.dma_start(go_row[:, :], row(g_o).broadcast_to([P, P])).then_inc(s_late, 16)
            sp.dma_start(bo_row[:, :], row(b_o).broadcast_to([P, P])).then_inc(s_late, 16)
            sp.dma_start(bias_row[:, :], row(expert_biases).broadcast_to([P, E])).then_inc(s_late, 16)
            sp.dma_start(cent[:, :], centroids).then_inc(s_late, 16)
            sp.dma_start(wsu[:, :], ws_up).then_inc(s_late, 16)
            sp.dma_start(wsd[:, :], ws_down).then_inc(s_late, 16)
            for half in range(2):
                sp.wait_ge(s_y, half + 1)
                sp.dma_start(out.rearrange("b (q p) d -> p (b q) d", p=P)[:, 4 * half:4 * half + 4, :],
                             y_out[:, 4 * half:4 * half + 4, :]).then_inc(s_out, 16)
            sp.wait_ge(s_out, 32)

        LATE = 16 * 7

        @block.gpsimd
        def _(pool):
            pool.memset(ident[:, :], 0.0).then_inc(s_pool, 1)
            pool.memset(one16[:, :], 0.0).then_inc(s_pool, 1)
            pool.memset(ident16[:, :], 0.0).then_inc(s_pool, 1)
            pool.memset(zeros16[:, :], 0.0).then_inc(s_pool, 1)
            pool.memset(wkT[:, :, :, :], 0.0).then_inc(s_pool, 1)
            pool.wait_ge(s_pool, 3)
            for m, fill in ((ident, 1.0), (one16, 1.0), (ident16, 1.0 / RANGE16)):
                pool.affine_select(out=m[:, :], in_=m[:, :], compare_op=ALU.not_equal, fill=fill,
                                   base=0, pattern=[[-1, P]], channel_multiplier=1).then_inc(s_pool, 1)

            pool.wait_ge(s_wvhi, 1)
            pool.tensor_tensor(wv_lo[:, :], wkv_s[:, INNER:2 * INNER], wv_hi[:, :].bitcast(F32),
                               ALU.subtract).then_inc(s_wvlo, 1)
            pool.wait_ge(s_wohi, 1)
            pool.tensor_tensor(w_all[:, :, 5, :], wo_s[:, :, :], w_all[:, :, 4, :].bitcast(F32),
                               ALU.subtract).then_inc(s_wolo, 1)
            for b in range(B // 2, B):
                pool.wait_ge(s_kvhi, b + 1)
                pool.tensor_tensor(kv_lo[:, b, :], kvT[:, b, :], kv_hi[:, b, :].bitcast(F32), ALU.subtract)\
                    .then_inc(s_kvlo, 1)

            def split_high(pr, step_in_pair, t, guard=True):
                if t % 2 == 0:
                    pool.wait_ge(s_rinv, pr * (2 * B) + (step_in_pair * 2 + t // 2 + 1))
                if guard:
                    pool.wait_ge(s_pT, pr * (B * TILES) + ((step_in_pair - 1) * TILES + t + 1))
                pool.tensor_tensor(p_hi[:, t, :], prob[:, t, :],
                                   p_rinv[:, t:t + 1].broadcast_to([P, KEYS]), ALU.mult).then_inc(s_phi, 1)

            for t in range(TILES):
                split_high(0, 0, t, guard=False)
            with pool.Fori(0, PAIRS - 1) as pr:
                for b in range(B):
                    for t in range(TILES):
                        split_high(pr, b + 1, t)
            for b in range(B - 1):
                for t in range(TILES):
                    split_high(PAIRS - 1, b + 1, t)

            pool.wait_ge(s_late, LATE)
            pool.tensor_tensor(x_res[:, :, :], x_res[:, :, :],
                               bo_row[:, :].unsqueeze(1).broadcast_to([P, NT, P]), ALU.add).then_inc(s_xres, 1)

            for b in range(B):
                pool.wait_ge(s_vst[b], 16 * PAIRS)
            pool.memset(sel16[:, :, :], 0.0).then_inc(s_sel, 1)
            pool.wait_ge(s_sel, 1)
            for part in range(2):
                pool.affine_select(out=sel16[:, :, :], in_=sel16[:, :, :], compare_op=ALU.not_equal,
                                   fill=1.0 / RANGE16, base=-part * E, pattern=[[-1, E], [0, FF]],
                                   channel_multiplier=1).then_inc(s_sel, 1)
                pool.wait_ge(s_sel, part + 2)

            pool.wait_ge(s_wup, 16 * PAIRS)
            pool.wait_ge(s_wdn, 16 * PAIRS)
            pool.wait_ge(s_wout, PAIRS * B + 1)

            up_cols = wup_s[:, :, :].rearrange("p e f -> p (e f)")
            down_cols = wdn_s[:, :, :].rearrange("p t d -> p (t d)")

            def split(w, hi, lo, f, n, done):
                pool.tensor_copy(hi, w[:, bass.ds(f * P, P)]).then_inc(s_pchain, 1)
                pool.wait_ge(s_pchain, n + 1)
                pool.sem_inc(s_held, 1)
                pool.tensor_tensor(lo, w[:, bass.ds(f * P, P)], hi.bitcast(F32), ALU.subtract)\
                    .then_inc(done, 1)

            def split_up(f, u, n, guard=True):
                if guard:
                    pool.wait_ge(s_u, f - 1)
                split(up_cols, wu_hi[:, u, :], wu_lo[:, u, :], f, n, s_wu)

            def split_down(f, u, n, guard=True):
                if guard:
                    pool.wait_ge(s_down, f - 1)
                split(down_cols, wd_hi[:, u, :], wd_lo[:, u, :], f, n, s_wd)

            split_up(0, 0, 0, guard=False)
            split_up(1, 1, 1, guard=False)
            split_up(2, 0, 2)
            split_down(0, 0, 3, guard=False)
            split_up(3, 1, 4)
            split_down(1, 1, 5, guard=False)
            with pool.Fori(1, FT // 2 - 1) as i:
                split_up(i * 2 + 2, 0, i * 4 + 2)
                split_down(i * 2, 0, i * 4 + 3)
                split_up(i * 2 + 3, 1, i * 4 + 4)
                split_down(i * 2 + 1, 1, i * 4 + 5)
            split_down(FT - 2, 0, 2 * FT - 2)
            split_down(FT - 1, 1, 2 * FT - 1)

        @block.scalar
        def _(act):
            act.dma_start(wkv_s[:, 0:INNER], wkv[:, 0:INNER]).then_inc(s_wk, 16)
            act.dma_start(wq_s[:, :], wq).then_inc(s_wq, 16)
            act.dma_start(wkv_s[:, INNER:2 * INNER], wkv[:, INNER:2 * INNER]).then_inc(s_wv, 16)
            act.dma_start(wo_s[:, :, :], wout.rearrange("(r p) d -> p r d", p=P)).then_inc(s_wo, 16)

            def root(half):
                act.wait_ge(s_var, half + 1)
                act.activation(rs[:, half * NT:(half + 1) * NT], tmp[:, 0, half * NT:(half + 1) * NT], ACT.Sqrt)\
                    .then_inc(s_std, 1)

            def evac_wk(g):
                act.wait_ge(s_tp, g + 1)
                for head in range(2):
                    cut = slice(head * DH, (head + 1) * DH)
                    act.activation(wkT[cut, 4 * g:4 * g + 4, head, :],
                                   ps[cut, SCORE_BANK + g, :].rearrange("p (r c) -> p r c", r=4),
                                   ACT.Copy).then_inc(s_wT, 1)

            def evac_wq(g):
                act.wait_ge(s_tp, g + 3)
                act.activation(wqT[:, 4 * g:4 * g + 4, :],
                               ps[:, SCORE_BANK + 2 + g, :].rearrange("p (r c) -> p r c", r=4),
                               ACT.Copy).then_inc(s_wT, 1)

            def normalise_context(b):
                if b % 2 == 0:
                    act.wait_ge(s_shift, b // 2 + 1)
                for q in range(QT):
                    j = b // 2 * NT + 4 + b % 2 * QT + q
                    ins = act.activation(tok[:, b, q, :], tok[:, b, q, :], ACT.Identity,
                                         bias=shift[:, j:j + 1], scale=rs[:, j:j + 1])
                    ins.then_inc(s_tokc, 1)

            def m_high(g):
                act.wait_ge(s_m, g + 1)
                act.activation(w_all[:, 2 * g:2 * g + 2, 0:2, :],
                               ps[:, SCORE_BANK + g, :].rearrange("p (r k c) -> p r k c", r=2, k=2),
                               ACT.Copy).then_inc(s_mhi, 1)

            def evac_tokens(b):
                act.wait_ge(s_kvtp, b + 1)
                for part in range(2):
                    act.activation(kvT[:, b, part * S:(part + 1) * S],
                                   ps[:, AV_BANK + b % 2, part * S:(part + 1) * S], ACT.Identity,
                                   bias=cols[:, 2 * part + 1:2 * part + 2],
                                   scale=cols[:, 2 * part:2 * part + 1]).then_inc(s_kvT, 1)

            act.wait_ge(s_pool, 5)
            evac_wk(0)
            evac_wk(1)
            evac_wq(0)
            evac_wq(1)
            act.wait_ge(s_wv, 16)
            act.activation(wv_hi[:, :], wkv_s[:, INNER:2 * INNER], ACT.Copy).then_inc(s_wvhi, 1)
            root(0)
            act.wait_ge(s_wo, 16)
            act.activation(w_all[:, :, 4, :], wo_s[:, :, :], ACT.Copy).then_inc(s_wohi, 1)
            root(1)
            m_high(0)
            normalise_context(0)
            normalise_context(1)
            m_high(1)
            m_high(2)
            act.wait_ge(s_cols, 64)
            evac_tokens(0)
            evac_tokens(1)
            normalise_context(2)
            normalise_context(3)
            m_high(3)
            evac_tokens(2)
            evac_tokens(3)

            def exp(k, t, guard=True):
                act.wait_ge(s_masked, k + 1)
                if guard:
                    act.wait_ge(s_plo, k - (TILES - 1))
                act.activation(prob[:, t, :], sc[:, t % 2, :], ACT.Exp, bias=neg_max[:, t:t + 1],
                               scale=-1.0, accum_out=p_sum[:, t:t + 1]).then_inc(s_exp, 1)

            def evac_t(k, step, t):
                act.wait_ge(s_pT, k + 1)
                if t == 0:
                    act.wait_ge(s_av, step + 1)
                head, qt = t // QT, t % QT
                act.activation(probT[:, head, :, qt * P:(qt + 1) * P],
                               ps[:, T_BANK + t % 2, :].rearrange("p (k c) -> p k c", k=KT),
                               ACT.Copy).then_inc(s_pTsb, 1)

            def ao_high(step):
                act.wait_ge(s_av, step + 2)
                act.wait_ge(s_wout, step + 1)
                act.activation(ao_hi[:, :], ps[:, AV_BANK, 0:S], ACT.Copy).then_inc(s_aohi, 1)

            def q_high(c, quarter, bank=Q_BANK):
                act.wait_ge(s_q, c + 1)
                head, half = quarter % 2, quarter // 2
                act.activation(q_hi[:, head, half * 512:(half + 1) * 512], ps[:, bank, :],
                               ACT.Copy).then_inc(s_qhi, 1)

            for what, n in OPENING:
                if what == "v" and n % 2 == 0:
                    act.wait_ge(s_v, n + 1)
                    act.activation(v_all[:, n // 2, 0:512], ps[:, V_BANKS[n % 4], :], ACT.Copy)\
                        .then_inc(s_vact, 1)
                elif what == "q":
                    q_high(n, n, T_BANK + n % 2)
                elif what == "x":
                    exp(n, n, guard=False)

            def pair_body(pr, last):
                for b in range(B):
                    step = pr * B + b
                    k = pr * (B * TILES) + b * TILES
                    more = not (last and b == B - 1)
                    evac_t(k, step, 0)
                    for t in range(1, TILES):
                        evac_t(k + t, step, t)
                        if more:
                            exp(k + (TILES + t - 1), t - 1)
                    if more:
                        exp(k + (2 * TILES - 1), TILES - 1)
                    if not last:
                        q_high(pr * 4 + (4 + b), b)
                    ao_high(step)

            act.sem_inc(s_pTsb, 2)
            with act.Fori(0, PAIRS - 1) as pr:
                pair_body(pr, False)
            pair_body(PAIRS - 1, True)

            act.wait_ge(s_wout, PAIRS * B + 1)
            act.activation(outT[:, 512:1024], ps[:, OUT_BANK + 1, :], ACT.Copy).then_inc(s_outT, 1)
            for n in range(2):
                act.wait_ge(s_var2, n + 1)
                act.activation(rs[:, 0:NT], tmp[:, 0, 0:NT], ACT.Sqrt).then_inc(s_std2, 1)
            for half in range(2):
                act.wait_ge(s_xhT, half + 1)
                act.activation(xfT[:, half * 512:(half + 1) * 512], ps[:, 4 + half, :], ACT.Copy)\
                    .then_inc(s_xfT, 1)
            for half in range(2):
                act.wait_ge(s_xfT, half + 1)
                act.activation(xf_hi[:, half * 512:(half + 1) * 512], xfT[:, half * 512:(half + 1) * 512],
                               ACT.Copy).then_inc(s_xfhi, 1)
            act.wait_ge(s_affsb, 1)
            act.activation(gate[:, :, :], aff[:, :, :], ACT.Exp, scale=-1.0).then_inc(s_eneg, 1)
            act.wait_ge(s_su, 1)
            act.activation(h[0:FF, 0, :].rearrange("p (a c) -> p a c", a=2), ps[0:FF, U_BANK:U_BANK + 2, :],
                           ACT.Silu).then_inc(s_ssilu, 1)
            act.wait_ge(s_ssilu, 1)
            act.activation(h_hi[0:FF, 0, :], h[0:FF, 0, :], ACT.Copy).then_inc(s_shi, 1)

            def silu(f, u, guard=True):
                act.wait_ge(s_u, f + 1)
                if guard:
                    act.wait_ge(s_hlo, f - 1)
                act.activation(h[:, u, :].rearrange("p (a c) -> p a c", a=2),
                               ps[:, U_BANK + 2 * u:U_BANK + 2 * u + 2, :], ACT.Silu).then_inc(s_silu, 1)

            def h_high(f, u, guard=True):
                act.wait_ge(s_h, f + 1)
                if guard:
                    act.wait_ge(s_down, f - 1)
                act.activation(h_hi[:, u, :], h[:, u, :], ACT.Copy).then_inc(s_hhi, 1)

            act.wait_ge(s_sd, 1)
            silu(0, 0, guard=False)
            silu(1, 1, guard=False)
            h_high(0, 0, guard=False)
            silu(2, 0)
            h_high(1, 1, guard=False)
            with act.Fori(0, FT // 2 - 2) as i:
                silu(i * 2 + 3, 1)
                h_high(i * 2 + 2, 0)
                silu(i * 2 + 4, 0)
                h_high(i * 2 + 3, 1)
            silu(FT - 1, 1)
            h_high(FT - 2, 0)
            h_high(FT - 1, 1)
            act.wait_ge(s_down, FT)
            act.activation(yT[:, 512:1024], ps[:, Y_BANK + 1, :], ACT.Copy).then_inc(s_yT, 1)

        @block.tensor
        def _(pe):
            def three(o, a_hi, a_lo, b_hi, b_lo, start=True, stop=True):
                skip = not (start and stop)
                pe.matmul(o, a_hi, b_hi, start=start, stop=False, skip_group_check=skip)
                pe.matmul(o, a_hi, b_lo, start=False, stop=False, skip_group_check=skip)
                return pe.matmul(o, a_lo, b_hi, start=False, stop=stop, skip_group_check=skip)

            pe.wait_ge(s_pool, 8)
            for g, (w, loaded) in enumerate(((wkv_s, s_wk), (wkv_s, s_wk), (wq_s, s_wq), (wq_s, s_wq))):
                pe.wait_ge(loaded, 16)
                for j in range(4):
                    r = 4 * (g % 2) + j
                    mm = pe.transpose(ps[:, SCORE_BANK + g, j * P:(j + 1) * P], w[:, r * P:(r + 1) * P],
                                      ident[:, :])
                mm.then_inc(s_tp, 1)

            def transpose_tokens(b):
                pe.wait_ge(s_tok, b + 1)
                pe.wait_ge(s_tokc, QT * (b + 1))
                if b >= 2:
                    pe.wait_ge(s_kvT, 2 * (b - 1))
                for j in range(KT):
                    mm = pe.transpose(ps[:, AV_BANK + b % 2, j * P:(j + 1) * P], tok[:, b, j, :],
                                      ident[:, :])
                mm.then_inc(s_kvtp, 1)

            pe.wait_ge(s_wT, 6)
            for g in range(PAIRS // 2):
                for j in range(2):
                    r = 2 * g + j
                    mm = pe.matmul(ps[:, SCORE_BANK + g, j * 256:(j + 1) * 256], wqT[:, r, :],
                                   wkT[:, r, :, :], start=True, stop=True)
                mm.then_inc(s_m, 1)
            transpose_tokens(0)
            transpose_tokens(1)
            transpose_tokens(2)
            transpose_tokens(3)

            def queries(c, quarter, bank=Q_BANK):
                head, half = quarter % 2, quarter // 2
                rows = slice(2 * half, 2 * half + 2)
                three(ps[:, bank, :].rearrange("p (b s) -> p b s", b=2),
                      m_st[:, head, :], m_st[:, 2 + head, :],
                      kv_hi[:, rows, S:2 * S], kv_lo[:, rows, S:2 * S]).then_inc(s_q, 1)

            def scores(b, t):
                head, qt = t // QT, t % QT
                at = b * S + qt * P
                three(ps[:, SCORE_BANK + t % 2, :], q_hi[:, head, at:at + P], q_lo[:, head, at:at + P],
                      kv_hi[:, b, :], kv_lo[:, b, :]).then_inc(s_score, 1)

            pe.wait_ge(s_wvlo, 1)
            for what, n in OPENING:
                if what == "v":
                    b, j, half = n // (2 * KT), n // 2 % KT, n % 2
                    if n % (2 * KT) == 0:
                        pe.wait_ge(s_kvlo, b + 1)
                    if n == 2:
                        pe.wait_ge(s_kvT, 2 * B)
                    if n >= 4:
                        pe.wait_ge(s_vdve if n % 2 else s_vact, n // 2 - 1)
                    cut = slice(half * 512, (half + 1) * 512)
                    three(ps[:, V_BANKS[n % 4], :], kv_hi[:, b, j * P:(j + 1) * P],
                          kv_lo[:, b, j * P:(j + 1) * P], wv_hi[:, cut], wv_lo[:, cut]).then_inc(s_v, 1)
                elif what == "q":
                    if n == 0:
                        pe.wait_ge(s_kvlo, B)
                        pe.wait_ge(s_mst, 16)
                        pe.wait_ge(s_mlo, PAIRS // 2)
                    if n >= 2:
                        pe.wait_ge(s_qlo, n - 1)
                    queries(n, n, T_BANK + n % 2)
                elif what == "s":
                    if n == 0:
                        pe.wait_ge(s_qlo, 4)
                    if n >= 2:
                        pe.wait_ge(s_masked, n - 1)
                    scores(0, n)
            pe.wait_ge(s_vact, B * KT)
            pe.wait_ge(s_vdve, B * KT)
            for n in range(2):
                mm = pe.matmul(ps[:, OUT_BANK + n, :], zeros16[:, 0:P], zeros16[:, :], start=True, stop=True)
            mm.then_inc(s_wout, 1)
            pe.sem_inc(s_av, 1)

            def transpose_p(k, t):
                pe.wait_ge(s_plo, k + 1)
                pe.wait_ge(s_pTsb, k + 1)
                for j in range(KT):
                    cut = slice(j * P, (j + 1) * P)
                    o = ps[:, T_BANK + t % 2, cut]
                    pe.matmul(o, p_hi[:, t, cut], ident16[:, :], start=True, stop=False)
                    mm = pe.matmul(o, p_lo[:, t, cut], ident16[:, :], start=False, stop=True)
                mm.then_inc(s_pT, 1)

            def attend(pr, step, b):
                pe.wait_ge(s_pTsb, step * TILES + (TILES + 2))
                pe.wait_ge(s_vst[b], pr * 16 + 16)
                pe.wait_ge(s_aolo, step + 1)
                for j in range(KT):
                    for head in range(2):
                        cut = slice(head * DH, (head + 1) * DH)
                        mm = pe.matmul(ps[cut, AV_BANK, 0:S], v_st[:, b, j, cut], probT[:, head, j, :],
                                       start=(j == 0), stop=(j == KT - 1), skip_group_check=True)
                mm.then_inc(s_av, 1)

            def project(step, b):
                pe.wait_ge(s_aolo, step + 2)
                at = b * S
                three(ps[:, OUT_BANK + at // 512, at % 512:at % 512 + S], wo_st[:, 0, :], wo_st[:, 1, :],
                      ao_hi[:, :], ao_lo[:, :], start=False, stop=False).then_inc(s_wout, 1)

            def pair_body(pr, first, last):
                for b in range(B):
                    step = pr * B + b
                    k = pr * (B * TILES) + b * TILES
                    more = not (last and b == B - 1)
                    for t in range(TILES):
                        transpose_p(k + t, t)
                        if t == 1 and not (first and b == 0):
                            if b == 1:
                                pe.wait_ge(s_wst, pr * 16 + 16)
                            project(step - 1, (b - 1) % B)
                        if more:
                            pe.wait_ge(s_masked, k + (TILES + t - 1))
                            if t == 0 and b == B - 1:
                                pe.wait_ge(s_qlo, pr * 4 + 6)
                            if t == 0 and b == 1:
                                pe.wait_ge(s_qlo, pr * 4 + 4)
                            scores((b + 1) % B, t)
                    if not last:
                        pe.wait_ge(s_mst, pr * 16 + 32)
                        pe.wait_ge(s_qlo, pr * 4 + (4 + b))
                        queries(pr * 4 + (4 + b), b)
                    attend(pr, step, b)

            pair_body(0, True, False)
            with pe.Fori(1, PAIRS - 1) as pr:
                pair_body(pr, False, False)
            pair_body(PAIRS - 1, False, True)
            project(PAIRS * B - 1, B - 1)

            for g in range(2):
                pe.wait_ge(s_outT, 2)
                for j in range(4):
                    mm = pe.transpose(ps[:, 2 + g, j * P:(j + 1) * P],
                                      outT[:, (4 * g + j) * P:(4 * g + j + 1) * P], ident[:, :])
                mm.then_inc(s_outTt, 1)
            pe.wait_ge(s_late, LATE)
            pe.transpose(ps[:, 6, 0:E], cent[:, :], ident[0:E, 0:E]).then_inc(s_cent, 1)
            pe.wait_ge(s_xh, 1)
            for g in range(2):
                for j in range(4):
                    mm = pe.transpose(ps[:, 4 + g, j * P:(j + 1) * P], xh[:, 4 * g + j, :], ident[:, :])
                mm.then_inc(s_xhT, 1)
            pe.wait_ge(s_centT, 1)
            pe.wait_ge(s_xfT, 2)
            for j in range(NT):
                mm = pe.matmul(ps[:, 7, j * E:(j + 1) * E], xfT[:, j * P:(j + 1) * P], centT[:, :],
                               start=True, stop=True)
            mm.then_inc(s_aff, 1)
            pe.wait_ge(s_xflo, 2)
            pe.wait_ge(s_sw, 4)
            for half in range(2):
                cut = slice(half * 512, (half + 1) * 512)
                mm = three(ps[0:FF, U_BANK + half, :], wsu_hi[:, :], wsu_lo[:, :], xf_hi[:, cut], xf_lo[:, cut])
            mm.then_inc(s_su, 1)

            def up(f, u):
                pe.wait_ge(s_wu, f + 1)
                for half in range(2):
                    cut = slice(half * 512, (half + 1) * 512)
                    mm = three(ps[:, U_BANK + 2 * u + half, :], wu_hi[:, u, :], wu_lo[:, u, :],
                               xf_hi[:, cut], xf_lo[:, cut])
                mm.then_inc(s_u, 1)

            def spread(f, guard=True):
                if guard:
                    pe.wait_ge(s_h, f)
                w = sel16[:, :, :].rearrange("p e f -> p (e f)")[:, bass.ds(f * P, P)]
                for half in range(2):
                    mm = pe.matmul(ps[:, CW_BANK + half, :], w, cwT16[:, half * 512:(half + 1) * 512],
                                   start=True, stop=True)
                mm.then_inc(s_cwb, 1)

            def down(f, u):
                pe.wait_ge(s_hlo, f + 1)
                pe.wait_ge(s_wd, f + 1)
                for half in range(2):
                    cut = slice(half * 512, (half + 1) * 512)
                    mm = three(ps[:, Y_BANK + half, :], wd_hi[:, u, :], wd_lo[:, u, :],
                               h_hi[:, u, cut], h_lo[:, u, cut], start=False, stop=False)
                mm.then_inc(s_down, 1)

            pe.wait_ge(s_slo, 1)
            for half in range(2):
                cut = slice(half * 512, (half + 1) * 512)
                o = ps[:, Y_BANK + half, :]
                pe.matmul(o, wsd_hi[:, :], h_hi[0:FF, 0, cut], start=True, stop=False, skip_group_check=True)
                pe.matmul(o, wsd_hi[:, :], h_lo[0:FF, 0, cut], start=False, stop=False, skip_group_check=True)
                mm = pe.matmul(o, wsd_lo[:, :], h_hi[0:FF, 0, cut], start=False, stop=False,
                               skip_group_check=True)
            mm.then_inc(s_sd, 1)
            up(0, 0)
            up(1, 1)
            pe.wait_ge(s_cw, 1)
            pe.wait_ge(s_affsb, 1)
            t16 = ps[:, CW_BANK, :].bitcast(F16)
            for j in range(NT):
                mm = pe.transpose(t16[:, j * P:(j + 1) * P], cw16[:, j, :, :].rearrange("p a e -> p (a e)"), one16[:, :])
            mm.then_inc(s_cwt, 1)
            pe.wait_ge(s_sel, 3)
            pe.wait_ge(s_cwT, 1)
            spread(0, guard=False)
            spread(1)

            def slot(f, u):
                pe.wait_ge(s_silu, f + 1)
                up(f + 2, u)
                spread(f + 2)
                down(f, u)

            with pe.Fori(0, FT // 2 - 1) as i:
                slot(i * 2, 0)
                slot(i * 2 + 1, 1)
            down(FT - 2, 0)
            down(FT - 1, 1)
            pe.wait_ge(s_yT, 2)
            for g in range(2):
                for j in range(4):
                    mm = pe.transpose(ps[:, 2 + g, j * P:(j + 1) * P],
                                      yT[:, (4 * g + j) * P:(4 * g + j + 1) * P], ident[:, :])
                mm.then_inc(s_yt, 1)


        @block.vector
        def _(dve):
            count = [0]

            def chain(ins):
                ins.then_inc(s_dve, 1)
                count[0] += 1

            def chained():
                dve.wait_ge(s_dve, count[0])

            chain(dve.memset(mask_add[:, :, S:KEYS], 0.0))

            def inverse_std(w, done, at=0):
                r, v, t = rs[:, at:at + w], tmp[:, 0, at:at + w], tmp[:, 1, at:at + w]
                dve.wait_ge(*done)
                chain(dve.reciprocal(r, r))
                chained()
                chain(dve.tensor_tensor(t, r, r, ALU.mult))
                chained()
                chain(dve.tensor_tensor(t, t, v, ALU.mult))
                chained()
                chain(dve.tensor_scalar(t, t, -0.5, 1.5, ALU.mult, ALU.add))
                chained()
                chain(dve.tensor_tensor(r, r, t, ALU.mult))
                chained()

            def moments(tiles, at=0):
                for j, tile in enumerate(tiles, at):
                    chain(dve.bn_stats(stats[:, j, :], tile))
                chained()
                for j in range(at, at + len(tiles)):
                    chain(dve.bn_aggr(mv[:, j, :], stats[:, j, :]))
                chained()

            def normalise(o, tile, j):
                return dve.tensor_scalar(o, tile, mv[:, j, 0:1], rs[:, j:j + 1], ALU.subtract, ALU.mult)

            def spread_of(half):
                at = half * NT
                dve.wait_ge(s_x[half], 32)
                moments([x_in[:, 4 * half + j, :] for j in range(4)], at)
                dve.wait_ge(s_ctx[half], 32)
                moments([tok[:, 2 * half + b, q, :] for b in range(2) for q in range(QT)], at + 4)
                chain(dve.tensor_scalar(tmp[:, 0, at:at + 4], mv[:, at:at + 4, 1], 1.0 + EPS, EPS * EPS,
                                        ALU.mult, ALU.add))
                chained()
                dve.tensor_scalar(tmp[:, 0, at + 4:at + NT], mv[:, at + 4:at + NT, 1], EPS, None, ALU.add)\
                   .then_inc(s_var, 1)

            def normalise_half(half):
                at = half * NT
                inverse_std(NT, (s_std, half + 1), at)
                dve.scalar_tensor_tensor(out=shift[:, at + 4:at + NT], in0=mv[:, at + 4:at + NT, 0], scalar=-1.0,
                                         in1=rs[:, at + 4:at + NT], op0=ALU.mult, op1=ALU.mult)\
                   .then_inc(s_shift, 1)
                for b in (2 * half, 2 * half + 1):
                    for q in range(QT):
                        j = at + b % 2 * QT + q
                        ins = normalise(tok[:, b, QT + q, :], x_in[:, QT * b + q, :], j)
                        if q == 0:
                            chain(ins)
                    ins.then_inc(s_tok, 1)

            def split_tokens(b):
                dve.wait_ge(s_kvT, 2 * (b + 1))
                dve.tensor_copy(kv_hi[:, b, :], kvT[:, b, :]).then_inc(s_kvhi, 1)
                if b >= B // 2:
                    return
                dve.wait_ge(s_kvhi, b + 1)
                dve.tensor_tensor(kv_lo[:, b, :], kvT[:, b, :], kv_hi[:, b, :].bitcast(F32), ALU.subtract)\
                   .then_inc(s_kvlo, 1)

            def m_low(g):
                dve.wait_ge(s_mhi, g + 1)
                dve.tensor_tensor(w_all[:, 2 * g:2 * g + 2, 2:4, :],
                                  ps[:, SCORE_BANK + g, :].rearrange("p (r k c) -> p r k c", r=2, k=2),
                                  w_all[:, 2 * g:2 * g + 2, 0:2, :].bitcast(F32), ALU.subtract)\
                   .then_inc(s_mlo, 1)

            spread_of(0)
            spread_of(1)
            normalise_half(0)
            normalise_half(1)
            dve.wait_ge(s_mask, 16)
            dve.tensor_scalar(mask_add[:, :, 0:S], mask_u8[:, :, :], -MASKED, MASKED, ALU.mult, ALU.add)\
               .then_inc(s_maskadd, 1)
            split_tokens(0)
            split_tokens(1)
            for g in range(PAIRS // 2):
                m_low(g)
            split_tokens(2)
            split_tokens(3)

            def mask_scores(k, t, guard=True):
                dve.wait_ge(s_score, k + 1)
                if guard:
                    dve.wait_ge(s_exp, k - 1)
                dve.sem_inc(s_held, 1)
                return dve.tensor_tensor_reduce(sc[:, t % 2, :], ps[:, SCORE_BANK + t % 2, :],
                                                mask_now, -SCALE, -LEAST, ALU.add, ALU.min,
                                                neg_max[:, t:t + 1]).then_inc(s_masked, 1)

            def invert(kk, t):
                dve.wait_ge(s_exp, kk * 2 + 2)
                dve.tensor_scalar(p_scaled[:, t:t + 2], p_sum[:, t:t + 2], 1.0 / RANGE16, None, ALU.mult)\
                   .then_inc(s_scaled, 1)
                dve.wait_ge(s_scaled, kk + 1)
                dve.reciprocal(p_rinv[:, t:t + 2], p_scaled[:, t:t + 2]).then_inc(s_rinv, 1)

            def split_low(k, t):
                dve.wait_ge(s_phi, k + 1)
                dve.scalar_tensor_tensor(out=p_lo[:, t, :], in0=prob[:, t, :], scalar=p_rinv[:, t:t + 1],
                                         in1=p_hi[:, t, :], op0=ALU.mult, op1=ALU.subtract)\
                   .then_inc(s_plo, 1)

            def ao_low(step):
                dve.wait_ge(s_aohi, step + 1)
                dve.tensor_tensor(ao_lo[:, :], ps[:, AV_BANK, 0:S], ao_hi[:, :].bitcast(F32),
                                  ALU.subtract).then_inc(s_aolo, 1)

            def q_low(c, quarter, bank=Q_BANK):
                dve.wait_ge(s_qhi, c + 1)
                head, half = quarter % 2, quarter // 2
                cut = slice(half * 512, (half + 1) * 512)
                dve.tensor_tensor(q_lo[:, head, cut], ps[:, bank, :], q_hi[:, head, cut].bitcast(F32),
                                  ALU.subtract).then_inc(s_qlo, 1)

            dve.wait_ge(s_maskadd, 1)
            chained()
            mask_now = mask_add[:, 0, :]
            for what, n in OPENING:
                if what == "v" and n % 2:
                    dve.wait_ge(s_v, n + 1)
                    dve.tensor_copy(v_all[:, n // 2, 512:1024], ps[:, V_BANKS[n % 4], :]).then_inc(s_vdve, 1)
                elif what == "q":
                    q_low(n, n, T_BANK + n % 2)
                elif what == "s":
                    mask_scores(n, n, guard=n >= 2)
                elif what == "i":
                    invert(n // 2, n)
                elif what == "lo":
                    split_low(n, n)

            def pair_body(pr, last):
                nonlocal mask_now
                for b in range(B):
                    step = pr * B + b
                    k = pr * (B * TILES) + (b + 1) * TILES
                    kk = pr * (B * 2) + (b + 1) * 2
                    more = not (last and b == B - 1)
                    mask_now = mask_add[:, (b + 1) % B, :]
                    if more:
                        mask_scores(k, 0)
                    split_low(k - 1, 3)
                    if more:
                        mask_scores(k + 1, 1)
                        mask_scores(k + 2, 2)
                        invert(kk, 0)
                        mask_scores(k + 3, 3)
                        split_low(k, 0)
                        invert(kk + 1, 2)
                        split_low(k + 1, 1)
                    if not last:
                        q_low(pr * 4 + (4 + b), b)
                    ao_low(step)
                    if more:
                        split_low(k + 2, 2)

            dve.sem_inc(s_aolo, 1)
            with dve.Fori(0, PAIRS - 1) as pr:
                pair_body(pr, False)
            pair_body(PAIRS - 1, True)

            dve.wait_ge(s_wout, PAIRS * B + 1)
            dve.tensor_copy(outT[:, 0:512], ps[:, OUT_BANK, :]).then_inc(s_outT, 1)
            dve.wait_ge(s_late, LATE)
            dve.tensor_copy(wsu_hi[:, :], wsu[:, :]).then_inc(s_sw, 1)
            dve.tensor_copy(wsd_hi[:, :], wsd[:, :]).then_inc(s_sw, 1)
            dve.wait_ge(s_sw, 2)
            dve.tensor_tensor(wsu_lo[:, :], wsu[:, :], wsu_hi[:, :].bitcast(F32), ALU.subtract).then_inc(s_sw, 1)
            dve.tensor_tensor(wsd_lo[:, :], wsd[:, :], wsd_hi[:, :].bitcast(F32), ALU.subtract).then_inc(s_sw, 1)
            turned = [ps[:, 2 + j // 4, j % 4 * P:(j % 4 + 1) * P] for j in range(NT)]
            dve.wait_ge(s_outTt, 2)
            moments(turned)
            dve.tensor_scalar(tmp[:, 0, 0:NT], mv[:, 0:NT, 1], EPS, None, ALU.add).then_inc(s_var2, 1)
            inverse_std(NT, (s_std2, 1))
            for j in range(NT):
                chain(dve.scalar_tensor_tensor(out=x1[:, j, :], in0=turned[j], scalar=mv[:, j, 0:1],
                                               in1=go_row[:, :], op0=ALU.subtract, op1=ALU.mult))
            dve.wait_ge(s_xres, 1)
            chained()
            for j in range(NT):
                chain(dve.scalar_tensor_tensor(out=x1[:, j, :], in0=x1[:, j, :], scalar=rs[:, j:j + 1],
                                               in1=x_res[:, j, :], op0=ALU.mult, op1=ALU.add))
            chained()
            moments([x1[:, j, :] for j in range(NT)])
            dve.tensor_scalar(tmp[:, 0, 0:NT], mv[:, 0:NT, 1], EPS, None, ALU.add).then_inc(s_var2, 1)
            inverse_std(NT, (s_std2, 2))
            for j in range(NT):
                ins = normalise(xh[:, j, :], x1[:, j, :], j)
                if j < NT - 1:
                    chain(ins)
            ins.then_inc(s_xh, 1)
            dve.wait_ge(s_cent, 1)
            dve.tensor_copy(centT[:, :], ps[:, 6, 0:E]).then_inc(s_centT, 1)
            for half in range(2):
                cut = slice(half * 512, (half + 1) * 512)
                dve.wait_ge(s_xfhi, half + 1)
                dve.tensor_tensor(xf_lo[:, cut], xfT[:, cut], xf_hi[:, cut].bitcast(F32), ALU.subtract)\
                   .then_inc(s_xflo, 1)
            dve.wait_ge(s_aff, 1)
            dve.tensor_copy(aff[:, :, :], ps[:, 7, :].rearrange("p (j e) -> p j e", j=NT)).then_inc(s_affsb, 1)
            dve.wait_ge(s_affsb, 1)
            chain(dve.tensor_tensor(biased[:, :, :], aff[:, :, :],
                                    bias_row[:, :].unsqueeze(1).broadcast_to([P, NT, E]), ALU.add))
            chained()
            for j in range(NT):
                chain(dve.max(top8[:, j, :], biased[:, j, :]))
            chained()
            for j in range(NT):
                chain(dve.match_replace(left[:, j, :], top8[:, j, :], biased[:, j, :], LEAST))
            chained()
            chain(dve.tensor_tensor(biased[:, :, :], left[:, :, :], biased[:, :, :], ALU.not_equal))
            dve.wait_ge(s_eneg, 1)
            chain(dve.tensor_scalar(gate[:, :, :], gate[:, :, :], 1.0, None, ALU.add))
            chained()
            chain(dve.reciprocal(gate[:, :, :], gate[:, :, :]))
            chained()
            chain(dve.tensor_tensor(gate[:, :, :], gate[:, :, :], biased[:, :, :], ALU.mult))
            chained()
            chain(dve.tensor_reduce(w_sum[:, 0, :], gate[:, :, :], AX_X, ALU.add))
            chained()
            chain(dve.tensor_scalar(w_sum[:, 0, :], w_sum[:, 0, :], COMBINE_EPS, 1.0 / RANGE16, ALU.add, ALU.mult))
            chained()
            chain(dve.reciprocal(w_sum[:, 1, :], w_sum[:, 0, :]))
            chained()
            chain(dve.tensor_tensor(combine[:, :, :], gate[:, :, :],
                                    w_sum[:, 1, :].unsqueeze(2).broadcast_to([P, NT, E]), ALU.mult))
            chained()
            chain(dve.tensor_copy(cw16[:, :, 0, :], combine[:, :, :]))
            chained()
            dve.tensor_tensor(cw16[:, :, 1, :], combine[:, :, :], cw16[:, :, 0, :], ALU.subtract)\
               .then_inc(s_cw, 1)
            dve.wait_ge(s_shi, 1)
            dve.tensor_tensor(h_lo[0:FF, 0, :], h[0:FF, 0, :], h_hi[0:FF, 0, :].bitcast(F32), ALU.subtract)\
               .then_inc(s_slo, 1)
            dve.wait_ge(s_cwt, 1)
            dve.tensor_copy(cwT16[:, :], ps[:, CW_BANK, :].bitcast(F16)).then_inc(s_cwT, 1)

            def weigh(f, u):
                dve.wait_ge(s_silu, f + 1)
                dve.wait_ge(s_cwb, f + 1)
                hv = h[:, u, :].rearrange("p (a c) -> p a c", a=2)
                dve.tensor_tensor(hv, hv, ps[:, CW_BANK:CW_BANK + 2, :], ALU.mult).then_inc(s_h, 1)

            def h_low(f, u):
                dve.wait_ge(s_hhi, f + 1)
                dve.tensor_tensor(h_lo[:, u, :], h[:, u, :], h_hi[:, u, :].bitcast(F32), ALU.subtract)\
                   .then_inc(s_hlo, 1)

            weigh(0, 0)
            weigh(1, 1)
            h_low(0, 0)
            with dve.Fori(0, FT // 2 - 1) as i:
                weigh(i * 2 + 2, 0)
                h_low(i * 2 + 1, 1)
                weigh(i * 2 + 3, 1)
                h_low(i * 2 + 2, 0)
            h_low(FT - 1, 1)
            dve.wait_ge(s_down, FT)
            dve.tensor_copy(yT[:, 0:512], ps[:, Y_BANK, :]).then_inc(s_yT, 1)
            for half in range(2):
                dve.wait_ge(s_yt, half + 1)
                dve.tensor_tensor(y_out[:, 4 * half:4 * half + 4, :],
                                  ps[:, 2 + half, :].rearrange("p (j d) -> p j d", j=4),
                                  x1[:, 4 * half:4 * half + 4, :], ALU.add).then_inc(s_y, 1)


INPUTS = ["x", "ctx_1024", "mask_BxS2_bf1", "L0_xattn_g_x", "L0_xattn_b_x", "L0_xattn_g_l", "L0_xattn_b_l",
          "L0_xattn_Wq", "L0_xattn_Wkv", "L0_xattn_Wout", "L0_xattn_g_o", "L0_xattn_b_o",
          "L0_ffn_centroids", "L0_ffn_expert_biases", "L0_ffn_Ws_up", "L0_ffn_Ws_down", "L0_ffn_W_up",
          "L0_ffn_W_down"]


def kernel(**inputs):
    import numpy as np
    import concourse.bacc as bacc
    from concourse.bass_utils import run_bass_kernel_spmd

    nc = bacc.Bacc("TRN2", target_bir_lowering=False, num_devices=1)
    arrays, args = {}, []
    for name in INPUTS:
        a = np.ascontiguousarray(inputs[name])
        if a.dtype == np.bool_:
            a = a.view(np.uint8)
        arrays["in_" + name] = a
        args.append(nc.dram_tensor("in_" + name, a.shape, mybir.dt.from_np(a.dtype), kind="ExternalInput").ap())
    shape = inputs["x"].shape
    args.append(nc.dram_tensor("out_0", shape, F32, kind="ExternalOutput").ap())
    xattn_moe(nc, *args)
    r = run_bass_kernel_spmd(nc, [arrays], core_ids=[0])
    return r.results[0]["out_0"]
```

```python
from contextlib import ExitStack

import concourse.bass as bass
from concourse import mybir

F32 = mybir.dt.float32
F32R = mybir.dt.float32r
F16 = mybir.dt.float16
U8 = mybir.dt.uint8
ALU = mybir.AluOpType
ACT = mybir.ActivationFunctionType
AX_X = mybir.AxisListType.X

P = 128
EPS = 1e-5
COMBINE_EPS = 1e-8
TOP_K = 8
MASKED = -1e30
LEAST = -3.0e38
RANGE16 = 4096.0


def xattn_moe(nc, x, ctx_in, mask, g_x, b_x, g_l, b_l, wq, wkv, wout, g_o, b_o,
              centroids, expert_biases, ws_up, ws_down, w_up, w_down, out):
    B, S, D = x.shape
    T = B * S
    NT = T // P
    KEYS = 2 * S
    KT = KEYS // P
    QT = S // P
    DH = 64
    INNER = wq.shape[1]
    PAIRS = INNER // (2 * DH)
    SCALE = DH ** -0.5
    E, _, FF = w_up.shape
    FT = E * FF // P
    TILES = 2 * QT
    LEAD = 6
    assert D == P and TILES == 4 and KEYS == 512 and NT == 8 and LEAD % 2 == 0

    stack = ExitStack()
    with stack:
        def sem(name):
            return stack.enter_context(nc.semaphore(name))

        def lay(offset, specs):
            made = []
            for name, shape, dt in specs:
                size = 4 if dt in (F32, F32R) else 2 if dt == F16 else 1
                for n in shape[1:]:
                    size *= n
                made.append(nc.alloc_sbuf_tensor_at(name, shape, dt, offset=offset))
                offset += (size + 31) // 32 * 32
            return made, offset

        base = (nc.sbuf_base + 31) // 32 * 32
        (ident, one16, ident16, zeros16, cols, stats, mv, rs, shift, tmp, neg_max, p_sum, p_scaled, p_rinv,
         ), top = lay(base, [
            ("ident", [P, P], F32), ("one16", [P, P], F16), ("ident16", [P, P], F16), ("zeros16", [P, 512], F16),
            ("cols", [P, 4], F32), ("stats", [P, 2 * NT, 6], F32), ("mv", [P, 2 * NT, 2], F32),
            ("rs", [P, 2 * NT], F32), ("shift", [P, 2 * NT], F32), ("tmp", [P, 2, 2 * NT], F32),
            ("neg_max", [P, TILES], F32), ("p_sum", [P, TILES], F32), ("p_scaled", [P, TILES], F32), ("p_rinv", [P, TILES], F32),
        ])
        step_base = top
        (tok, x_in, kvT, wqT, wkT), end1 = lay(step_base, [
            ("tok", [P, B, KT, P], F32), ("x_in", [P, NT, P], F32), ("kvT", [P, B, KEYS], F32),
            ("wqT", [P, PAIRS, P], F32), ("wkT", [P, PAIRS, 2, P], F32),
        ])
        (sc, prob, p_hi, p_lo, probT, ao_hi, ao_lo), end2 = lay(step_base, [
            ("sc", [P, 2, KEYS], F32), ("prob", [P, TILES, KEYS], F32),
            ("p_hi", [P, TILES, KEYS], F16), ("p_lo", [P, TILES, KEYS], F16),
            ("probT", [P, 2, KT, S], F32), ("ao_hi", [P, S], F32R), ("ao_lo", [P, S], F32R),
        ])
        v_base = max(end1, end2)
        (v_all, w_all, kv_hi, kv_lo, q_hi, q_lo, m_st, wo_st, v_st, mask_add), raw_base = lay(v_base, [
            ("v_all", [P, B * KT, INNER], F32),
            ("w_all", [P, PAIRS, 6, P], F32R),
            ("kv_hi", [P, B, KEYS], F32R), ("kv_lo", [P, B, KEYS], F32R),
            ("q_hi", [P, 2, T], F32R), ("q_lo", [P, 2, T], F32R),
            ("m_st", [P, 4, P], F32R), ("wo_st", [P, 2, P], F32R),
            ("v_st", [P, B, KT, P], F32), ("mask_add", [P, B, KEYS], F32),
        ])
        v_end = v_base + B * KT * INNER * 4
        (wq_s, wkv_s, wv_hi, wv_lo, wo_s, mask_u8), end1 = lay(raw_base, [
            ("wq_s", [P, INNER], F32), ("wkv_s", [P, 2 * INNER], F32),
            ("wv_hi", [P, INNER], F32R), ("wv_lo", [P, INNER], F32R),
            ("wo_s", [P, PAIRS, P], F32), ("mask_u8", [P, B, S], U8),
        ])
        (wup_s, wdn_s), end2 = lay(raw_base, [
            ("wup_s", [P, E, FF], F32), ("wdn_s", [P, FT, P], F32),
        ])
        (x_res, go_row, bo_row, bias_row, cent, centT, wsu, wsd, wsd_hi, wsd_lo, w_sum, top8, x1, xf_hi,
         xf_lo), h_base = lay(v_base, [
            ("x_res", [P, NT, P], F32), ("go_row", [P, P], F32), ("bo_row", [P, P], F32),
            ("bias_row", [P, E], F32), ("cent", [E, P], F32), ("centT", [P, E], F32),
            ("wsu", [P, FF], F32), ("wsd", [FF, P], F32), ("wsd_hi", [FF, P], F32R), ("wsd_lo", [FF, P], F32R),
            ("w_sum", [P, 2, NT], F32), ("top8", [P, NT, 8], F32), ("x1", [P, NT, P], F32),
            ("xf_hi", [P, T], F32R), ("xf_lo", [P, T], F32R),
        ])
        (h,), h_end = lay(h_base, [("h", [P, FT, T], F32)])
        over = -(-(h_end - raw_base) // (P * 4))
        assert over <= FT - LEAD and h_base + T * 4 <= v_end
        (outT,), _ = lay(h_base, [("outT", [P, T], F32)])
        (yT, y_out, last_hi, last_lo, last_wd_hi, last_wd_lo), last_end = lay(h_base, [
            ("yT", [P, T], F32), ("y_out", [P, NT, P], F32),
            ("last_hi", [P, LEAD, T], F32R), ("last_lo", [P, LEAD, T], F32R),
            ("last_wd_hi", [P, LEAD, P], F32R), ("last_wd_lo", [P, LEAD, P], F32R),
        ])
        LAST = FT - LEAD
        UNDER = -(-(last_end - h_base) // (T * 4))
        assert UNDER + LEAD < LAST
        SCRATCH = 10
        (xh, xfT, hs, biased, left, gate, combine, cw16), end3 = lay(h_base + (FT - SCRATCH) * T * 4, [
            ("xh", [P, NT, P], F32), ("xfT", [P, T], F32), ("hs", [FF, T], F32),
            ("biased", [P, NT, E], F32), ("left", [P, NT, E], F32),
            ("gate", [P, NT, E], F32), ("combine", [P, NT, E], F32), ("cw16", [P, NT, 2, E], F16),
        ])
        assert SCRATCH <= FT - LEAD and end3 <= raw_base
        (sel16, h_hi, h_lo, cwT16, wd_hi, wd_lo, wu_hi, wu_lo, wsu_hi, wsu_lo), end3 = lay(step_base, [
            ("sel16", [P, E, FF], F16), ("h_hi", [P, 2, T], F32R), ("h_lo", [P, 2, T], F32R),
            ("cwT16", [P, T], F16), ("wd_hi", [P, 2, P], F32R), ("wd_lo", [P, 2, P], F32R),
            ("wu_hi", [P, 2, P], F32R), ("wu_lo", [P, 2, P], F32R),
            ("wsu_hi", [P, FF], F32R), ("wsu_lo", [P, FF], F32R),
        ])
        assert end3 <= v_base

        ps = stack.enter_context(nc.psum_tensor("ps", [P, 8, 512], F32))
        OUT_BANK, SCORE_BANK, T_BANK, AV_BANK, Q_BANK = 0, 2, 4, 6, 7
        U_BANK, CW_BANK, Y_BANK = 2, 6, 0

        def v_bank(n):
            return (0, 1)[n % 2] if n < 8 else (0, 1, 6, 7)[n % 4]

        def v_before(n):
            return max((m for m in range(n) if v_bank(m) == v_bank(n)), default=None)

        CHUNKS = 2 * B * KT
        between = {1: ["t2"], 2: ["m1"], 3: ["t3", "m2"], 5: ["m3"], 7: ["q0"], 8: ["q1"], 9: ["q2"], 10: ["q3"], 13: ["s0"], 14: ["s1", "x0"], 16: ["x1"],
                   17: ["s2", "i0"], 18: ["s3", "x2"], 20: ["x3"], 21: ["lo0"], 22: ["i2"], 23: ["lo1"],
                   26: ["lo2"]}
        OPENING = [item for n in range(CHUNKS) for item in [f"v{n}"] + between.get(n, [])]
        OPENING = [(item.rstrip("0123456789"), int(item.lstrip("vtmqsxilo"))) for item in OPENING]

        CLOSING = LAST - 10
        halves = [(what, tile, half) for f in range(CLOSING, FT) for what, tile in (("up", f + LEAD), ("down", f))
                  for half in range(2) if tile < FT]
        spread_at = {3 * n: CLOSING + 2 + n for n in range(FT - 3 - CLOSING)}
        spread_at[3 * len(spread_at) + 2] = FT - 1
        closing = []
        for n, item in enumerate(halves):
            if n in spread_at:
                closing.append(("spread", spread_at[n], 0))
            closing.append(item)
        closing_low = []
        for what, tile, half in closing:
            if what == "spread":
                closing_low.append(("weigh", tile))
            elif what == "down" and half == 0:
                if tile + 1 < LAST:
                    closing_low.append(("low", tile + 1))
                if LAST <= tile + 2 < FT:
                    closing_low.append(("low", tile + 2))

        s_x = [sem("s_x0"), sem("s_x1")]
        s_ctx = [sem("s_ctx0"), sem("s_ctx1")]
        s_cols, s_mask = sem("s_cols"), sem("s_mask")
        s_wq, s_wk, s_wv, s_wo = sem("s_wq"), sem("s_wk"), sem("s_wv"), sem("s_wo")
        s_late = sem("s_late")
        s_wup, s_wdn = sem("s_wup"), sem("s_wdn")
        s_mst, s_wst = sem("s_mst"), sem("s_wst")
        s_vst = [sem(f"s_vst{b}") for b in range(B)]
        s_pool = sem("s_pool")
        s_dve = sem("s_dve")
        s_table = sem("s_table")
        s_var, s_std = sem("s_var"), sem("s_std")
        s_tok, s_tokc = sem("s_tok"), sem("s_tokc")
        s_shift, s_shift2 = sem("s_shift"), sem("s_shift2")
        s_tp, s_kvtp = sem("s_tp"), sem("s_kvtp")
        s_wT = sem("s_wT")
        s_kvT, s_kvhi, s_kvlo = sem("s_kvT"), sem("s_kvhi"), sem("s_kvlo")
        s_m, s_mhi, s_mlo = sem("s_m"), sem("s_mhi"), sem("s_mlo")
        s_wvhi, s_wvlo = sem("s_wvhi"), sem("s_wvlo")
        s_wohi, s_wolo = sem("s_wohi"), sem("s_wolo")
        s_v, s_vact, s_vdve = sem("s_v"), sem("s_vact"), sem("s_vdve")
        s_maskadd = sem("s_maskadd")
        s_held = sem("s_held")
        s_score, s_masked, s_exp = sem("s_score"), sem("s_masked"), sem("s_exp")
        s_scaled, s_rinv = sem("s_scaled"), sem("s_rinv")
        s_phi, s_plo, s_pT, s_pTsb = sem("s_phi"), sem("s_plo"), sem("s_pT"), sem("s_pTsb")
        s_av, s_aohi, s_aolo, s_wout = sem("s_av"), sem("s_aohi"), sem("s_aolo"), sem("s_wout")
        s_q, s_qhi, s_qlo = sem("s_q"), sem("s_qhi"), sem("s_qlo")
        s_outT, s_outTt, s_d2 = sem("s_outT"), sem("s_outTt"), sem("s_d2")
        s_var2, s_std2 = sem("s_var2"), sem("s_std2")
        s_biased = sem("s_biased")
        s_xh, s_xhT, s_xfT, s_xfhi, s_xflo = (sem("s_xh"), sem("s_xhT"), sem("s_xfT"), sem("s_xfhi"),
                                              sem("s_xflo"))
        s_cent, s_centT, s_aff, s_sigmoid = sem("s_cent"), sem("s_centT"), sem("s_aff"), sem("s_sigmoid")
        s_xres = sem("s_xres")
        s_cw, s_cwt, s_cwT, s_sel = sem("s_cw"), sem("s_cwt"), sem("s_cwT"), sem("s_sel")
        s_sw, s_su, s_ssilu, s_shi, s_slo, s_sd = (sem("s_sw"), sem("s_su"), sem("s_ssilu"),
                                                   sem("s_shi"), sem("s_slo"), sem("s_sd"))
        s_wu, s_wd, s_pchain = sem("s_wu"), sem("s_wd"), sem("s_pchain")
        s_u, s_cwb, s_silu, s_h, s_hhi, s_hlo, s_down = (sem("s_u"), sem("s_cwb"), sem("s_silu"),
                                                         sem("s_h"), sem("s_hhi"), sem("s_hlo"),
                                                         sem("s_down"))
        s_last = sem("s_last")
        s_yT, s_yt, s_y, s_out = [sem("s_yT0"), sem("s_yT1")], sem("s_yt"), sem("s_y"), sem("s_out")

        def row(v):
            return v.rearrange("(a d) -> a d", a=1)

        def col(v):
            return v.rearrange("(d a) -> d a", a=1)

        h_all = h[:, :, :].rearrange("p f t -> p (f t)")

        block = stack.enter_context(nc.Block())

        @block.sync
        def _(sp):
            def load_tokens(half):
                two = slice(2 * half, 2 * half + 2)
                sp.dma_start(x_in[:, QT * 2 * half:QT * 2 * (half + 1), :],
                             x[two, :, :].rearrange("b (q p) d -> p (b q) d", p=P)).then_inc(s_x[half], 16)
                for b in (2 * half, 2 * half + 1):
                    sp.dma_start(tok[:, b, 0:QT, :],
                                 ctx_in[b, :, :].rearrange("(q p) d -> p q d", p=P)).then_inc(s_ctx[half], 16)

            load_tokens(0)
            load_tokens(1)
            for i, v in enumerate((g_x, b_x, g_l, b_l)):
                sp.dma_start(cols[:, i:i + 1], col(v)).then_inc(s_cols, 16)
            sp.dma_start(wo_s[:, :, :], wout.rearrange("(r p) d -> p r d", p=P)).then_inc(s_wo, 16)
            sp.dma_start(mask_u8[:, :, :],
                         mask.rearrange("(o b) s -> o b s", o=1).broadcast_to([P, B, S])).then_inc(s_mask, 16)

            def stage_m(pair):
                sp.dma_start(m_st[:, :, :].bitcast(F32), w_all[:, bass.ds(pair, 1), 0:4, :]
                             .rearrange("p a k c -> p (a k) c").bitcast(F32)).then_inc(s_mst, 16)

            def stage_wo(pair):
                sp.dma_start(wo_st[:, :, :].bitcast(F32), w_all[:, bass.ds(pair, 1), 4:6, :]
                             .rearrange("p a k c -> p (a k) c").bitcast(F32)).then_inc(s_wst, 16)

            def stage_v(pair, b):
                sp.dma_start(v_st[:, b, :, :], v_all[:, b * KT:(b + 1) * KT, bass.ds(pair * P, P)])\
                    .then_inc(s_vst[b], 16)

            sp.wait_ge(s_mlo, 1)
            stage_m(0)
            for b in range(B):
                sp.wait_ge(s_vact, (b + 1) * KT)
                sp.wait_ge(s_vdve, (b + 1) * KT)
                stage_v(0, b)

            def load_experts(part):
                sp.dma_start(wup_s[:, bass.ds(part * (E // PAIRS), E // PAIRS), :],
                             w_up[bass.ds(part * (E // PAIRS), E // PAIRS), :, :].rearrange("e d f -> d e f"))\
                    .then_inc(s_wup, 16)
                sp.dma_start(wdn_s[:, bass.ds(part * (FT // PAIRS), FT // PAIRS), :],
                             w_down[bass.ds(part * (E // PAIRS), E // PAIRS), :, :]
                             .rearrange("(t two) f d -> (two f) t d", two=2)).then_inc(s_wdn, 16)

            sp.wait_ge(s_wolo, 1)
            with sp.Fori(0, PAIRS - 1) as pr:
                sp.wait_ge(s_q, (pr + 1) * 4)
                stage_m(pr + 1)
                sp.wait_ge(s_wout, pr * B + 1)
                stage_wo(pr)
                for b in range(B):
                    sp.wait_ge(s_av, pr * B + (b + 2))
                    stage_v(pr + 1, b)
                    if b == 0:
                        load_experts(pr)
            sp.wait_ge(s_wout, (PAIRS - 1) * B + 1)
            stage_wo(PAIRS - 1)
            load_experts(PAIRS - 1)
            for b in range(B):
                sp.wait_ge(s_vst[b], 16 * PAIRS)
            sp.dma_start(x_res[:, :, :], x.rearrange("b (q p) d -> p (b q) d", p=P)).then_inc(s_late, 16)
            sp.dma_start(go_row[:, :], row(g_o).broadcast_to([P, P])).then_inc(s_late, 16)
            sp.dma_start(bo_row[:, :], row(b_o).broadcast_to([P, P])).then_inc(s_late, 16)
            sp.dma_start(bias_row[:, :], row(expert_biases).broadcast_to([P, E])).then_inc(s_late, 16)
            sp.dma_start(cent[:, :], centroids).then_inc(s_late, 16)
            sp.dma_start(wsu[:, :], ws_up).then_inc(s_late, 16)
            sp.dma_start(wsd[:, :], ws_down).then_inc(s_late, 16)
            for half in range(2):
                sp.wait_ge(s_y, half + 1)
                sp.dma_start(out.rearrange("b (q p) d -> p (b q) d", p=P)[:, 4 * half:4 * half + 4, :],
                             y_out[:, 4 * half:4 * half + 4, :]).then_inc(s_out, 16)
            sp.wait_ge(s_out, 32)

        LATE = 16 * 7

        @block.gpsimd
        def _(pool):
            pool.memset(ident[:, :], 0.0).then_inc(s_pool, 1)
            pool.memset(one16[:, :], 0.0).then_inc(s_pool, 1)
            pool.memset(ident16[:, :], 0.0).then_inc(s_pool, 1)
            pool.memset(zeros16[:, :], 0.0).then_inc(s_pool, 1)
            pool.memset(wkT[:, :, :, :], 0.0).then_inc(s_pool, 1)
            pool.wait_ge(s_pool, 3)
            for m, fill in ((ident, 1.0), (one16, 1.0), (ident16, 1.0 / RANGE16)):
                pool.affine_select(out=m[:, :], in_=m[:, :], compare_op=ALU.not_equal, fill=fill,
                                   base=0, pattern=[[-1, P]], channel_multiplier=1).then_inc(s_pool, 1)

            pool.wait_ge(s_wvhi, 1)
            pool.tensor_tensor(wv_lo[:, :], wkv_s[:, INNER:2 * INNER], wv_hi[:, :].bitcast(F32),
                               ALU.subtract).then_inc(s_wvlo, 1)
            for b in range(B // 2, B):
                pool.wait_ge(s_kvhi, b + 1)
                pool.tensor_tensor(kv_lo[:, b, :], kvT[:, b, :], kv_hi[:, b, :].bitcast(F32), ALU.subtract)\
                    .then_inc(s_kvlo, 1)
            pool.wait_ge(s_wohi, 1)
            pool.tensor_tensor(w_all[:, :, 5, :], wo_s[:, :, :], w_all[:, :, 4, :].bitcast(F32),
                               ALU.subtract).then_inc(s_wolo, 1)

            def split_high(pr, step_in_pair, t, guard=True):
                if t % 2 == 0:
                    pool.wait_ge(s_rinv, pr * (2 * B) + (step_in_pair * 2 + t // 2 + 1))
                if guard:
                    pool.wait_ge(s_pT, pr * (B * TILES) + ((step_in_pair - 1) * TILES + t + 1))
                pool.tensor_tensor(p_hi[:, t, :], prob[:, t, :],
                                   p_rinv[:, t:t + 1].broadcast_to([P, KEYS]), ALU.mult).then_inc(s_phi, 1)

            for t in range(TILES):
                split_high(0, 0, t, guard=False)
            with pool.Fori(0, PAIRS - 1) as pr:
                for b in range(B):
                    for t in range(TILES):
                        split_high(pr, b + 1, t)
            for b in range(B - 1):
                for t in range(TILES):
                    split_high(PAIRS - 1, b + 1, t)

            pool.wait_ge(s_late, LATE)
            pool.tensor_tensor(x_res[:, :, :], x_res[:, :, :],
                               bo_row[:, :].unsqueeze(1).broadcast_to([P, NT, P]), ALU.add).then_inc(s_xres, 1)

            pool.wait_ge(s_wout, PAIRS * B + 1)
            pool.tensor_copy(wsu_hi[:, :], wsu[:, :]).then_inc(s_sw, 1)
            pool.tensor_copy(wsd_hi[:, :], wsd[:, :]).then_inc(s_sw, 1)
            pool.wait_ge(s_sw, 2)
            pool.tensor_tensor(wsu_lo[:, :], wsu[:, :], wsu_hi[:, :].bitcast(F32), ALU.subtract).then_inc(s_sw, 1)
            pool.tensor_tensor(wsd_lo[:, :], wsd[:, :], wsd_hi[:, :].bitcast(F32), ALU.subtract).then_inc(s_sw, 1)

            up_cols = wup_s[:, :, :].rearrange("p e f -> p (e f)")
            down_cols = wdn_s[:, :, :].rearrange("p t d -> p (t d)")

            def split(w, hi, lo, f, n, done):
                pool.tensor_copy(hi, w[:, bass.ds(f * P, P)]).then_inc(s_pchain, 1)
                pool.wait_ge(s_pchain, n + 1)
                pool.sem_inc(s_held, 1)
                pool.tensor_tensor(lo, w[:, bass.ds(f * P, P)], hi.bitcast(F32), ALU.subtract)\
                    .then_inc(done, 1)

            def split_up(f, u, n, guard=True):
                if guard:
                    pool.wait_ge(s_u, f - 1)
                split(up_cols, wu_hi[:, u, :], wu_lo[:, u, :], f, n, s_wu)

            def split_down(f, u, n, guard=True):
                if guard:
                    pool.wait_ge(s_down, f - 1)
                split(down_cols, wd_hi[:, u, :], wd_lo[:, u, :], f, n, s_wd)

            pool.wait_ge(s_wup, 16 * PAIRS)
            pool.wait_ge(s_wdn, 16 * PAIRS)
            split_up(0, 0, 0, guard=False)
            split_up(1, 1, 1, guard=False)

            pool.memset(sel16[:, :, :], 0.0).then_inc(s_sel, 1)
            split(up_cols, wd_hi[:, 0, :], wd_lo[:, 0, :], 2, 2, s_wu)
            pool.wait_ge(s_xfhi, 1)
            pool.tensor_tensor(xf_lo[:, 0:512], xfT[:, 0:512], xf_hi[:, 0:512].bitcast(F32), ALU.subtract)\
                .then_inc(s_xflo, 1)
            split(up_cols, wd_hi[:, 1, :], wd_lo[:, 1, :], 3, 3, s_wu)
            pool.wait_ge(s_sel, 1)
            for part in range(2):
                pool.affine_select(out=sel16[:, :, :], in_=sel16[:, :, :], compare_op=ALU.not_equal,
                                   fill=1.0 / RANGE16, base=-part * E, pattern=[[-1, E], [0, FF]],
                                   channel_multiplier=1).then_inc(s_sel, 1)
                pool.wait_ge(s_sel, part + 2)

            for f in range(4, LEAD):
                pool.wait_ge(s_u, f - 3)
                split_up(f, f % 2, f, guard=False)
            for f in range(2):
                split_up(f + LEAD, f % 2, LEAD + 2 * f)
                split_down(f, f % 2, LEAD + 2 * f + 1, guard=False)
            with pool.Fori(1, (FT - LEAD) // 2) as i:
                for u in range(2):
                    split_up(i * 2 + (u + LEAD), u, i * 4 + (LEAD + 2 * u))
                    split_down(i * 2 + u, u, i * 4 + (LEAD + 2 * u + 1))
            for f in range(LAST, FT):
                pool.tensor_copy(last_wd_hi[:, f - LAST, :], wdn_s[:, f, :]).then_inc(s_pchain, 1)
                pool.wait_ge(s_pchain, FT + f + 1)
                pool.tensor_tensor(last_wd_lo[:, f - LAST, :], wdn_s[:, f, :],
                                   last_wd_hi[:, f - LAST, :].bitcast(F32), ALU.subtract).then_inc(s_wd, 1)

        @block.scalar
        def _(act):
            act.dma_start(wkv_s[:, 0:INNER], wkv[:, 0:INNER]).then_inc(s_wk, 16)
            act.dma_start(wq_s[:, :], wq).then_inc(s_wq, 16)
            act.dma_start(wkv_s[:, INNER:2 * INNER], wkv[:, INNER:2 * INNER]).then_inc(s_wv, 16)

            def root(half):
                act.wait_ge(s_var, half + 1)
                act.activation(rs[:, half * NT:(half + 1) * NT], tmp[:, 0, half * NT:(half + 1) * NT], ACT.Sqrt)\
                    .then_inc(s_std, 1)

            def evac_wk(g):
                act.wait_ge(s_tp, g + 1)
                for head in range(2):
                    cut = slice(head * DH, (head + 1) * DH)
                    act.activation(wkT[cut, 4 * g:4 * g + 4, head, :],
                                   ps[cut, SCORE_BANK + g, :].rearrange("p (r c) -> p r c", r=4),
                                   ACT.Copy).then_inc(s_wT, 1)

            def evac_wq(g):
                act.wait_ge(s_tp, g + 3)
                act.activation(wqT[:, 4 * g:4 * g + 4, :],
                               ps[:, SCORE_BANK + 2 + g, :].rearrange("p (r c) -> p r c", r=4),
                               ACT.Copy).then_inc(s_wT, 1)

            def normalise_context(b):
                if b % 2 == 0:
                    act.wait_ge(s_shift, b // 2 + 1)
                for q in range(QT):
                    j = b // 2 * NT + 4 + b % 2 * QT + q
                    ins = act.activation(tok[:, b, q, :], tok[:, b, q, :], ACT.Identity,
                                         bias=shift[:, j:j + 1], scale=rs[:, j:j + 1])
                    ins.then_inc(s_tokc, 1)

            def m_high(g):
                act.wait_ge(s_m, g + 1)
                act.activation(w_all[:, 2 * g:2 * g + 2, 0:2, :],
                               ps[:, SCORE_BANK + g, :].rearrange("p (r k c) -> p r k c", r=2, k=2),
                               ACT.Copy).then_inc(s_mhi, 1)

            def evac_tokens(b):
                act.wait_ge(s_kvtp, b + 1)
                for part in range(2):
                    act.activation(kvT[:, b, part * S:(part + 1) * S],
                                   ps[:, AV_BANK + b % 2, part * S:(part + 1) * S], ACT.Identity,
                                   bias=cols[:, 2 * part + 1:2 * part + 2],
                                   scale=cols[:, 2 * part:2 * part + 1]).then_inc(s_kvT, 1)

            act.wait_ge(s_pool, 8)
            act.activation(tmp[:, 1, 0:1], ident[:, 0:1], ACT.Sqrt).then_inc(s_table, 1)
            evac_wk(0)
            evac_wk(1)
            root(0)
            evac_wq(0)
            evac_wq(1)
            act.wait_ge(s_wv, 16)
            act.activation(wv_hi[:, :], wkv_s[:, INNER:2 * INNER], ACT.Copy).then_inc(s_wvhi, 1)
            normalise_context(0)
            normalise_context(1)
            act.wait_ge(s_cols, 64)
            evac_tokens(0)
            root(1)
            evac_tokens(1)
            m_high(0)
            normalise_context(2)
            normalise_context(3)

            def exp(k, t, guard=True):
                act.wait_ge(s_masked, k + 1)
                if guard:
                    act.wait_ge(s_plo, k - (TILES - 1))
                act.activation(prob[:, t, :], sc[:, t % 2, :], ACT.Exp, bias=neg_max[:, t:t + 1],
                               scale=-1.0, accum_out=p_sum[:, t:t + 1]).then_inc(s_exp, 1)

            def evac_t(k, step, t):
                act.wait_ge(s_pT, k + 1)
                if t == 0:
                    act.wait_ge(s_av, step + 1)
                head, qt = t // QT, t % QT
                act.activation(probT[:, head, :, qt * P:(qt + 1) * P],
                               ps[:, T_BANK + t % 2, :].rearrange("p (k c) -> p k c", k=KT),
                               ACT.Copy).then_inc(s_pTsb, 1)

            def ao_high(step):
                act.wait_ge(s_av, step + 2)
                act.wait_ge(s_wout, step + 1)
                act.activation(ao_hi[:, :], ps[:, AV_BANK, 0:S], ACT.Copy).then_inc(s_aohi, 1)

            def q_high(c, quarter, bank=Q_BANK):
                act.wait_ge(s_q, c + 1)
                head, half = quarter % 2, quarter // 2
                act.activation(q_hi[:, head, half * 512:(half + 1) * 512], ps[:, bank, :],
                               ACT.Copy).then_inc(s_qhi, 1)

            for what, n in OPENING:
                if what == "v" and n % 2 == 0:
                    act.wait_ge(s_v, n + 1)
                    act.activation(v_all[:, n // 2, 0:512], ps[:, v_bank(n), :], ACT.Copy)\
                        .then_inc(s_vact, 1)
                elif what == "m":
                    m_high(n)
                elif what == "t":
                    evac_tokens(n)
                elif what == "q":
                    q_high(n, n, T_BANK + n % 2)
                elif what == "x":
                    exp(n, n, guard=False)
                    if n == 1:
                        act.wait_ge(s_wo, 16)
                        act.activation(w_all[:, :, 4, :], wo_s[:, :, :], ACT.Copy).then_inc(s_wohi, 1)

            def evac_out(half):
                act.wait_ge(s_wout, PAIRS * B - 1 + 2 * half)
                act.activation(outT[:, half * 512:(half + 1) * 512], ps[:, OUT_BANK + half, :], ACT.Copy)\
                    .then_inc(s_outT, 1)

            def root2(n, last):
                act.wait_ge(s_var2, last + 1)
                cut = slice(4 * n, 4 * last + 4)
                act.activation(rs[:, cut], tmp[:, 0, cut], ACT.Sqrt).then_inc(s_std2, 1)

            def pair_body(pr, last):
                for b in range(B):
                    step = pr * B + b
                    k = pr * (B * TILES) + b * TILES
                    more = not (last and b == B - 1)
                    evac_t(k, step, 0)
                    for t in range(1, TILES):
                        evac_t(k + t, step, t)
                        if last and b == B - 2 and t == TILES - 1:
                            evac_out(0)
                        if more:
                            exp(k + (TILES + t - 1), t - 1)
                    if more:
                        exp(k + (2 * TILES - 1), TILES - 1)
                    if not last:
                        q_high(pr * 4 + (4 + b), b)
                    if last and b == B - 1:
                        root2(0, 0)
                    ao_high(step)
                    if last and b == B - 2:
                        act.activation(cols[:, 0:1], ident[:, 0:1], ACT.Sqrt).then_inc(s_table, 1)

            with act.Fori(0, PAIRS - 1) as pr:
                pair_body(pr, False)
            pair_body(PAIRS - 1, True)

            evac_out(1)
            root2(1, 2)

            def evac_xf(half):
                act.wait_ge(s_xhT, half + 1)
                act.activation(xfT[:, half * 512:(half + 1) * 512], ps[:, 4 + half, :], ACT.Copy)\
                    .then_inc(s_xfT, 1)

            def xf_high(half):
                act.wait_ge(s_xfT, half + 1)
                act.activation(xf_hi[:, half * 512:(half + 1) * 512], xfT[:, half * 512:(half + 1) * 512],
                               ACT.Copy).then_inc(s_xfhi, 1)

            act.wait_ge(s_shift2, 1)
            for j in range(4):
                ins = act.activation(xh[:, j, :], x1[:, j, :], ACT.Identity, bias=shift[:, j:j + 1],
                                     scale=rs[:, 4 + j:5 + j])
            ins.then_inc(s_xh, 1)
            evac_xf(0)
            xf_high(0)
            root2(3, 3)
            evac_xf(1)
            xf_high(1)
            act.wait_ge(s_biased, 2)
            act.activation(gate[:, :, :].rearrange("p (a j) e -> p a (j e)", a=2), ps[:, 6:8, 0:4 * E],
                           ACT.Sigmoid).then_inc(s_sigmoid, 1)
            def shared_silu():
                act.wait_ge(s_su, 1)
                act.activation(hs[:, :].rearrange("p (a c) -> p a c", a=2), ps[0:FF, Y_BANK:Y_BANK + 2, :],
                               ACT.Silu).then_inc(s_ssilu, 1)

            def shared_high():
                act.wait_ge(s_ssilu, 1)
                act.activation(h_hi[0:FF, 1, :], hs[:, :], ACT.Copy).then_inc(s_shi, 1)

            def silu(f, u):
                act.wait_ge(s_u, f + 1)
                act.activation(h_all[:, bass.ds(f * T, T)].rearrange("p (a c) -> p a c", a=2),
                               ps[:, U_BANK + 2 * u:U_BANK + 2 * u + 2, :], ACT.Silu).then_inc(s_silu, 1)

            def h_high(f, u, guard=True):
                act.wait_ge(s_h, f + 1)
                if guard:
                    act.wait_ge(s_down, f - 1)
                act.activation(h_hi[:, u, :], h_all[:, bass.ds(f * T, T)], ACT.Copy).then_inc(s_hhi, 1)

            for f in range(LEAD - 1):
                silu(f, f % 2)
                if f == 1:
                    shared_silu()
                if f == 2:
                    shared_high()
            h_high(0, 0, guard=False)
            silu(LEAD - 1, 1)
            act.wait_ge(s_sd, 1)
            h_high(1, 1, guard=False)
            silu(LEAD, 0)
            h_high(2, 0)
            silu(LEAD + 1, 1)
            with act.Fori(1, LAST // 2 - 1) as i:
                h_high(i * 2 + 1, 1)
                silu(i * 2 + LEAD, 0)
                h_high(i * 2 + 2, 0)
                silu(i * 2 + (LEAD + 1), 1)
            h_high(LAST - 1, 1)
            silu(FT - 2, 0)
            for f in range(LAST, FT):
                act.wait_ge(s_h, f + 1)
                if f == LAST:
                    act.wait_ge(s_hlo, UNDER)
                act.activation(last_hi[:, f - LAST, :], h[:, f, :], ACT.Copy).then_inc(s_hhi, 1)
                if f == LAST + 2:
                    silu(FT - 1, 1)
            act.wait_ge(s_last, 2)
            act.activation(yT[:, 512:1024], ps[:, Y_BANK + 1, :], ACT.Copy).then_inc(s_yT[1], 1)

        @block.tensor
        def _(pe):
            def three(o, a_hi, a_lo, b_hi, b_lo, start=True, stop=True):
                skip = not (start and stop)
                pe.matmul(o, a_hi, b_hi, start=start, stop=False, skip_group_check=skip)
                pe.matmul(o, a_hi, b_lo, start=False, stop=False, skip_group_check=skip)
                return pe.matmul(o, a_lo, b_hi, start=False, stop=stop, skip_group_check=skip)

            pe.wait_ge(s_pool, 8)
            for g, (w, loaded) in enumerate(((wkv_s, s_wk), (wkv_s, s_wk), (wq_s, s_wq), (wq_s, s_wq))):
                pe.wait_ge(loaded, 16)
                for j in range(4):
                    r = 4 * (g % 2) + j
                    mm = pe.transpose(ps[:, SCORE_BANK + g, j * P:(j + 1) * P], w[:, r * P:(r + 1) * P],
                                      ident[:, :])
                mm.then_inc(s_tp, 1)

            def transpose_tokens(b):
                pe.wait_ge(s_tok, b + 1)
                pe.wait_ge(s_tokc, QT * (b + 1))
                if b >= 2:
                    pe.wait_ge(s_kvT, 2 * (b - 1))
                for j in range(KT):
                    mm = pe.transpose(ps[:, AV_BANK + b % 2, j * P:(j + 1) * P], tok[:, b, j, :],
                                      ident[:, :])
                mm.then_inc(s_kvtp, 1)

            pe.wait_ge(s_wT, 6)
            def head_matrices(g):
                for j in range(2):
                    r = 2 * g + j
                    mm = pe.matmul(ps[:, SCORE_BANK + g, j * 256:(j + 1) * 256], wqT[:, r, :],
                                   wkT[:, r, :, :], start=True, stop=True)
                mm.then_inc(s_m, 1)

            head_matrices(0)
            transpose_tokens(0)
            transpose_tokens(1)
            head_matrices(1)
            head_matrices(2)
            head_matrices(3)

            def queries(c, quarter, bank=Q_BANK):
                head, half = quarter % 2, quarter // 2
                rows = slice(2 * half, 2 * half + 2)
                three(ps[:, bank, :].rearrange("p (b s) -> p b s", b=2),
                      m_st[:, head, :], m_st[:, 2 + head, :],
                      kv_hi[:, rows, S:2 * S], kv_lo[:, rows, S:2 * S]).then_inc(s_q, 1)

            def scores(b, t):
                head, qt = t // QT, t % QT
                at = b * S + qt * P
                three(ps[:, SCORE_BANK + t % 2, :], q_hi[:, head, at:at + P], q_lo[:, head, at:at + P],
                      kv_hi[:, b, :], kv_lo[:, b, :]).then_inc(s_score, 1)

            pe.wait_ge(s_wvlo, 1)
            for what, n in OPENING:
                if what == "v":
                    b, j, half = n // (2 * KT), n // 2 % KT, n % 2
                    if n % (2 * KT) == 0:
                        pe.wait_ge(s_kvlo, b + 1)
                    if v_before(n) is not None:
                        pe.wait_ge(s_vdve if n % 2 else s_vact, v_before(n) // 2 + 1)
                    cut = slice(half * 512, (half + 1) * 512)
                    three(ps[:, v_bank(n), :], kv_hi[:, b, j * P:(j + 1) * P],
                          kv_lo[:, b, j * P:(j + 1) * P], wv_hi[:, cut], wv_lo[:, cut]).then_inc(s_v, 1)
                elif what == "t":
                    transpose_tokens(n)
                elif what == "q":
                    if n == 0:
                        pe.wait_ge(s_kvlo, B)
                        pe.wait_ge(s_mst, 16)
                        pe.wait_ge(s_mlo, PAIRS // 2)
                    if n >= 2:
                        pe.wait_ge(s_qlo, n - 1)
                    queries(n, n, T_BANK + n % 2)
                elif what == "s":
                    if n == 0:
                        pe.wait_ge(s_qlo, 4)
                    if n >= 2:
                        pe.wait_ge(s_masked, n - 1)
                    scores(0, n)
            pe.sem_inc(s_av, 1)

            def transpose_p(k, t):
                pe.wait_ge(s_plo, k + 1)
                if t >= 2:
                    pe.wait_ge(s_pTsb, k - 1)
                for j in range(KT):
                    cut = slice(j * P, (j + 1) * P)
                    o = ps[:, T_BANK + t % 2, cut]
                    pe.matmul(o, p_hi[:, t, cut], ident16[:, :], start=True, stop=False)
                    mm = pe.matmul(o, p_lo[:, t, cut], ident16[:, :], start=False, stop=True)
                mm.then_inc(s_pT, 1)

            def attend(pr, step, b):
                pe.wait_ge(s_pTsb, step * TILES + TILES)
                pe.wait_ge(s_vst[b], pr * 16 + 16)
                for j in range(KT):
                    for head in range(2):
                        cut = slice(head * DH, (head + 1) * DH)
                        mm = pe.matmul(ps[cut, AV_BANK, 0:S], v_st[:, b, j, cut], probT[:, head, j, :],
                                       start=(j == 0), stop=(j == KT - 1), skip_group_check=True)
                mm.then_inc(s_av, 1)

            def project(step, b):
                pe.wait_ge(s_aolo, step + 1)
                at = b * S
                three(ps[:, OUT_BANK + at // 512, at % 512:at % 512 + S], wo_st[:, 0, :], wo_st[:, 1, :],
                      ao_hi[:, :], ao_lo[:, :], start=False, stop=False).then_inc(s_wout, 1)

            def turn_out(half, bank):
                pe.wait_ge(s_outT, half + 1)
                for j in range(4):
                    at = (4 * half + j) * P
                    mm = pe.transpose(ps[:, bank, j * P:(j + 1) * P], outT[:, at:at + P], ident[:, :])
                mm.then_inc(s_outTt, 1)

            def pair_body(pr, first, last):
                for b in range(B):
                    step = pr * B + b
                    k = pr * (B * TILES) + b * TILES
                    more = not (last and b == B - 1)
                    for t in range(TILES):
                        transpose_p(k + t, t)
                        if t == 1 and first and b == 0:
                            pe.wait_ge(s_vact, B * KT)
                            pe.wait_ge(s_vdve, B * KT)
                            for n in range(2):
                                mm = pe.matmul(ps[:, OUT_BANK + n, :], zeros16[:, 0:P], zeros16[:, :],
                                               start=True, stop=True)
                            mm.then_inc(s_wout, 1)
                        elif t == 1:
                            if b == 1:
                                pe.wait_ge(s_wst, pr * 16 + 16)
                            project(step - 1, (b - 1) % B)
                        if more:
                            if t >= 2:
                                pe.wait_ge(s_masked, k + (TILES + t - 1))
                            if t == 0 and b == B - 1:
                                pe.wait_ge(s_qlo, pr * 4 + 6)
                            if t == 0 and b == 1:
                                pe.wait_ge(s_qlo, pr * 4 + 4)
                            scores((b + 1) % B, t)
                    if not last:
                        if b == 0:
                            pe.wait_ge(s_mst, pr * 16 + 32)
                        queries(pr * 4 + (4 + b), b)
                    attend(pr, step, b)
                    if last and b == B - 2:
                        turn_out(0, Q_BANK)

            pair_body(0, True, False)
            with pe.Fori(1, PAIRS - 1) as pr:
                pair_body(pr, False, False)
            pair_body(PAIRS - 1, False, True)
            project(PAIRS * B - 1, B - 1)

            pe.wait_ge(s_late, LATE)
            pe.transpose(ps[:, AV_BANK, 0:E], cent[:, :], ident[0:E, 0:E]).then_inc(s_cent, 1)
            turn_out(1, T_BANK + 1)
            def turn_input(half):
                pe.wait_ge(s_xh, half + 1)
                for j in range(4):
                    mm = pe.transpose(ps[:, 4 + half, j * P:(j + 1) * P], xh[:, 4 * half + j, :], ident[:, :])
                mm.then_inc(s_xhT, 1)

            def affinities(half):
                if half == 0:
                    pe.wait_ge(s_centT, 1)
                pe.wait_ge(s_xfT, half + 1)
                for j in range(4):
                    at = (4 * half + j) * P
                    mm = pe.matmul(ps[:, 6 + half, j * E:(j + 1) * E], xfT[:, at:at + P], centT[:, :],
                                   start=True, stop=True)
                mm.then_inc(s_aff, 1)

            def shared_up(half):
                cut = slice(half * 512, (half + 1) * 512)
                return three(ps[0:FF, Y_BANK + half, :], wsu_hi[:, :], wsu_lo[:, :],
                             xf_hi[:, cut], xf_lo[:, cut])

            def up_half(u, half, hi=wu_hi, lo=wu_lo):
                cut = slice(half * 512, (half + 1) * 512)
                return three(ps[:, U_BANK + 2 * u + half, :], hi[:, u, :], lo[:, u, :],
                             xf_hi[:, cut], xf_lo[:, cut])

            def up(f, u, hi=wu_hi, lo=wu_lo):
                pe.wait_ge(s_wu, f + 1)
                up_half(u, 0, hi, lo)
                up_half(u, 1, hi, lo).then_inc(s_u, 1)

            turn_input(0)
            affinities(0)
            pe.wait_ge(s_xflo, 1)
            pe.wait_ge(s_sw, 4)
            shared_up(0)
            turn_input(1)
            pe.wait_ge(s_wu, 2)
            up_half(0, 0)
            affinities(1)
            up_half(1, 0)
            pe.wait_ge(s_xflo, 2)
            shared_up(1).then_inc(s_su, 1)
            up_half(0, 1).then_inc(s_u, 1)
            up_half(1, 1).then_inc(s_u, 1)

            def spread(f, guard=True):
                if guard:
                    pe.wait_ge(s_h, f)
                w = sel16[:, :, :].rearrange("p e f -> p (e f)")[:, bass.ds(f * P, P)]
                for half in range(2):
                    mm = pe.matmul(ps[:, CW_BANK + half, :], w, cwT16[:, half * 512:(half + 1) * 512],
                                   start=True, stop=True)
                mm.then_inc(s_cwb, 1)

            def down_half(half, w_hi, w_lo, h_hi, h_lo):
                return three(ps[:, Y_BANK + half, :], w_hi, w_lo, h_hi, h_lo, start=False, stop=False)

            def down(f, u):
                pe.wait_ge(s_hlo, f + 1)
                pe.wait_ge(s_wd, f + 1)
                for half in range(2):
                    cut = slice(half * 512, (half + 1) * 512)
                    mm = down_half(half, wd_hi[:, u, :], wd_lo[:, u, :], h_hi[:, u, cut], h_lo[:, u, cut])
                mm.then_inc(s_down, 1)

            for f in range(2, LEAD):
                if f == LEAD - 2:
                    pe.wait_ge(s_cw, 1)
                    pe.wait_ge(s_sigmoid, 1)
                    t16 = ps[:, CW_BANK, :].bitcast(F16)
                    for j in range(NT):
                        mm = pe.transpose(t16[:, j * P:(j + 1) * P],
                                          cw16[:, j, :, :].rearrange("p a e -> p (a e)"), one16[:, :])
                    mm.then_inc(s_cwt, 1)
                if f == LEAD - 1:
                    pe.wait_ge(s_sel, 3)
                    pe.wait_ge(s_cwT, 1)
                    spread(0, guard=False)
                pe.wait_ge(s_silu, f - 1)
                if f < 4:
                    up(f, f % 2, wd_hi, wd_lo)
                else:
                    up(f, f % 2)
            spread(1)
            pe.wait_ge(s_slo, 1)
            for half in range(2):
                cut = slice(half * 512, (half + 1) * 512)
                o = ps[:, Y_BANK + half, :]
                pe.matmul(o, wsd_hi[:, :], h_hi[0:FF, 1, cut], start=True, stop=False, skip_group_check=True)
                pe.matmul(o, wsd_hi[:, :], h_lo[0:FF, 1, cut], start=False, stop=False, skip_group_check=True)
                mm = pe.matmul(o, wsd_lo[:, :], h_hi[0:FF, 1, cut], start=False, stop=False,
                               skip_group_check=True)
            mm.then_inc(s_sd, 1)

            with pe.Fori(0, CLOSING // 2) as i:
                for u in range(2):
                    f = i * 2 + u
                    spread(f + 2)
                    pe.wait_ge(s_silu, f + (LEAD - 1))
                    up(f + LEAD, u)
                    down(f, u)
            for what, f, half in closing:
                cut = slice(half * 512, (half + 1) * 512)
                if what == "spread":
                    spread(f)
                elif what == "up":
                    if half == 0:
                        pe.wait_ge(s_silu, f - 1)
                        pe.wait_ge(s_wu, f + 1)
                    mm = up_half(f % 2, half)
                    if half == 1:
                        mm.then_inc(s_u, 1)
                else:
                    if half == 0:
                        pe.wait_ge(s_hlo, f + 1)
                        pe.wait_ge(s_wd, f + 1)
                    if f < LAST:
                        mm = down_half(half, wd_hi[:, f % 2, :], wd_lo[:, f % 2, :],
                                       h_hi[:, f % 2, cut], h_lo[:, f % 2, cut])
                    else:
                        mm = down_half(half, last_wd_hi[:, f - LAST, :], last_wd_lo[:, f - LAST, :],
                                       last_hi[:, f - LAST, cut], last_lo[:, f - LAST, cut])
                    if f < LAST and half == 1:
                        mm.then_inc(s_down, 1)
                    if f == FT - 1:
                        mm.then_inc(s_last, 1)
            for g in range(2):
                pe.wait_ge(s_yT[g], 1)
                for j in range(4):
                    mm = pe.transpose(ps[:, 2 + g, j * P:(j + 1) * P],
                                      yT[:, (4 * g + j) * P:(4 * g + j + 1) * P], ident[:, :])
                mm.then_inc(s_yt, 1)


        @block.vector
        def _(dve):
            count = [0]

            def chain(ins):
                ins.then_inc(s_dve, 1)
                count[0] += 1

            def chained():
                dve.wait_ge(s_dve, count[0])

            chain(dve.memset(mask_add[:, :, S:KEYS], 0.0))

            def inverse_std(w, done, at=0):
                r, v, t = rs[:, at:at + w], tmp[:, 0, at:at + w], tmp[:, 1, at:at + w]
                dve.wait_ge(*done)
                chain(dve.reciprocal(r, r))
                chained()
                chain(dve.tensor_tensor(t, r, r, ALU.mult))
                chained()
                chain(dve.tensor_tensor(t, t, v, ALU.mult))
                chained()
                chain(dve.tensor_scalar(t, t, -0.5, 1.5, ALU.mult, ALU.add))
                chained()
                chain(dve.tensor_tensor(r, r, t, ALU.mult))
                chained()

            def moments(tiles, at=0):
                for j, tile in enumerate(tiles, at):
                    chain(dve.bn_stats(stats[:, j, :], tile))
                chained()
                for j in range(at, at + len(tiles)):
                    chain(dve.bn_aggr(mv[:, j, :], stats[:, j, :]))
                chained()

            def normalise(o, tile, j):
                return dve.tensor_scalar(o, tile, mv[:, j, 0:1], rs[:, j:j + 1], ALU.subtract, ALU.mult)

            def token_moments(half):
                dve.wait_ge(s_x[half], 16)
                moments([x_in[:, 4 * half + j, :] for j in range(4)], half * NT)

            def spread_of(half):
                at = half * NT
                dve.wait_ge(s_ctx[half], 32)
                moments([tok[:, 2 * half + b, q, :] for b in range(2) for q in range(QT)], at + 4)
                chain(dve.tensor_scalar(tmp[:, 0, at:at + 4], mv[:, at:at + 4, 1], 1.0 + EPS, EPS * EPS,
                                        ALU.mult, ALU.add))
                chained()
                dve.tensor_scalar(tmp[:, 0, at + 4:at + NT], mv[:, at + 4:at + NT, 1], EPS, None, ALU.add)\
                   .then_inc(s_var, 1)

            def normalise_half(half):
                at = half * NT
                inverse_std(NT, (s_std, half + 1), at)
                dve.scalar_tensor_tensor(out=shift[:, at + 4:at + NT], in0=mv[:, at + 4:at + NT, 0], scalar=-1.0,
                                         in1=rs[:, at + 4:at + NT], op0=ALU.mult, op1=ALU.mult)\
                   .then_inc(s_shift, 1)
                for b in (2 * half, 2 * half + 1):
                    for q in range(QT):
                        j = at + b % 2 * QT + q
                        ins = normalise(tok[:, b, QT + q, :], x_in[:, QT * b + q, :], j)
                        if q == 0:
                            chain(ins)
                    ins.then_inc(s_tok, 1)

            def split_tokens(b):
                dve.wait_ge(s_kvT, 2 * (b + 1))
                dve.tensor_copy(kv_hi[:, b, :], kvT[:, b, :]).then_inc(s_kvhi, 1)
                if b >= B // 2:
                    return
                dve.wait_ge(s_kvhi, b + 1)
                dve.tensor_tensor(kv_lo[:, b, :], kvT[:, b, :], kv_hi[:, b, :].bitcast(F32), ALU.subtract)\
                   .then_inc(s_kvlo, 1)

            def m_low(g):
                dve.wait_ge(s_mhi, g + 1)
                dve.tensor_tensor(w_all[:, 2 * g:2 * g + 2, 2:4, :],
                                  ps[:, SCORE_BANK + g, :].rearrange("p (r k c) -> p r k c", r=2, k=2),
                                  w_all[:, 2 * g:2 * g + 2, 0:2, :].bitcast(F32), ALU.subtract)\
                   .then_inc(s_mlo, 1)

            dve.wait_ge(s_table, 1)
            token_moments(0)
            spread_of(0)
            normalise_half(0)
            token_moments(1)
            spread_of(1)
            split_tokens(0)
            normalise_half(1)
            m_low(0)
            split_tokens(1)

            def mask_scores(k, t, guard=True):
                dve.wait_ge(s_score, k + 1)
                if guard:
                    dve.wait_ge(s_exp, k - 1)
                dve.sem_inc(s_held, 1)
                return dve.tensor_tensor_reduce(sc[:, t % 2, :], ps[:, SCORE_BANK + t % 2, :],
                                                mask_now, -SCALE, -LEAST, ALU.add, ALU.min,
                                                neg_max[:, t:t + 1]).then_inc(s_masked, 1)

            def invert(kk, t):
                dve.wait_ge(s_exp, kk * 2 + 2)
                dve.tensor_scalar(p_scaled[:, t:t + 2], p_sum[:, t:t + 2], 1.0 / RANGE16, None, ALU.mult)\
                   .then_inc(s_scaled, 1)
                dve.wait_ge(s_scaled, kk + 1)
                dve.reciprocal(p_rinv[:, t:t + 2], p_scaled[:, t:t + 2]).then_inc(s_rinv, 1)

            def split_low(k, t):
                dve.wait_ge(s_phi, k + 1)
                dve.scalar_tensor_tensor(out=p_lo[:, t, :], in0=prob[:, t, :], scalar=p_rinv[:, t:t + 1],
                                         in1=p_hi[:, t, :], op0=ALU.mult, op1=ALU.subtract)\
                   .then_inc(s_plo, 1)

            def ao_low(step):
                dve.wait_ge(s_aohi, step + 1)
                dve.tensor_tensor(ao_lo[:, :], ps[:, AV_BANK, 0:S], ao_hi[:, :].bitcast(F32),
                                  ALU.subtract).then_inc(s_aolo, 1)

            def q_low(c, quarter, bank=Q_BANK):
                dve.wait_ge(s_qhi, c + 1)
                head, half = quarter % 2, quarter // 2
                cut = slice(half * 512, (half + 1) * 512)
                dve.tensor_tensor(q_lo[:, head, cut], ps[:, bank, :], q_hi[:, head, cut].bitcast(F32),
                                  ALU.subtract).then_inc(s_qlo, 1)

            mask_now = mask_add[:, 0, :]
            for what, n in OPENING:
                if what == "v" and n % 2:
                    dve.wait_ge(s_v, n + 1)
                    dve.tensor_copy(v_all[:, n // 2, 512:1024], ps[:, v_bank(n), :]).then_inc(s_vdve, 1)
                elif what == "m":
                    m_low(n)
                elif what == "t":
                    split_tokens(n)
                elif what == "q":
                    q_low(n, n, T_BANK + n % 2)
                elif what == "s":
                    if n == 0:
                        dve.wait_ge(s_mask, 16)
                        dve.tensor_scalar(mask_add[:, :, 0:S], mask_u8[:, :, :], -MASKED, MASKED, ALU.mult, ALU.add)\
                           .then_inc(s_maskadd, 1)
                        dve.wait_ge(s_maskadd, 1)
                        chained()
                    mask_scores(n, n, guard=n >= 2)
                elif what == "i":
                    invert(n // 2, n)
                elif what == "lo":
                    split_low(n, n)

            turned = [[ps[:, bank, j * P:(j + 1) * P] for j in range(4)] for bank in (Q_BANK, T_BANK + 1)]

            def variances(n):
                half = n // 2
                if n % 2 == 0:
                    dve.wait_ge(s_outTt, half + 1)
                    moments(turned[half], 4 * n)
                else:
                    moments([x1[:, 4 * half + j, :] for j in range(4)], 4 * n)
                dve.tensor_scalar(tmp[:, 0, 4 * n:4 * n + 4], mv[:, 4 * n:4 * n + 4, 1], EPS, None, ALU.add)\
                   .then_inc(s_var2, 1)

            def centre_and_gain(half):
                n = 2 * half
                dve.wait_ge(s_late, LATE)
                for j in range(4):
                    chain(dve.scalar_tensor_tensor(out=x1[:, 4 * half + j, :], in0=turned[half][j],
                                                   scalar=mv[:, 4 * n + j, 0:1],
                                                   in1=go_row[:, :], op0=ALU.subtract, op1=ALU.mult))

            def residual(half):
                n = 2 * half
                dve.wait_ge(s_xres, 1)
                chained()
                for j in range(4):
                    chain(dve.scalar_tensor_tensor(out=x1[:, 4 * half + j, :], in0=x1[:, 4 * half + j, :],
                                                   scalar=rs[:, 4 * n + j:4 * n + j + 1],
                                                   in1=x_res[:, 4 * half + j, :], op0=ALU.mult, op1=ALU.add))
                chained()

            def expert_input():
                inverse_std(4, (s_std2, 3), 12)
                for j in range(4):
                    ins = normalise(xh[:, 4 + j, :], x1[:, 4 + j, :], 12 + j)
                    if j < 3:
                        chain(ins)
                ins.then_inc(s_xh, 1)

            def pair_body(pr, last):
                nonlocal mask_now
                for b in range(B):
                    step = pr * B + b
                    k = pr * (B * TILES) + (b + 1) * TILES
                    kk = pr * (B * 2) + (b + 1) * 2
                    more = not (last and b == B - 1)
                    mask_now = mask_add[:, (b + 1) % B, :]
                    if more:
                        mask_scores(k, 0)
                    split_low(k - 1, 3)
                    if more:
                        mask_scores(k + 1, 1)
                        mask_scores(k + 2, 2)
                        invert(kk, 0)
                        mask_scores(k + 3, 3)
                        split_low(k, 0)
                        invert(kk + 1, 2)
                        split_low(k + 1, 1)
                    if not last:
                        q_low(pr * 4 + (4 + b), b)
                    if last and b == B - 1:
                        variances(0)
                        inverse_std(4, (s_std2, 1), 0)
                        centre_and_gain(0)
                    ao_low(step)
                    if more:
                        split_low(k + 2, 2)

            with dve.Fori(0, PAIRS - 1) as pr:
                pair_body(pr, False)
            pair_body(PAIRS - 1, True)

            residual(0)
            variances(1)
            dve.wait_ge(s_cent, 1)
            dve.tensor_copy(centT[:, :], ps[:, AV_BANK, 0:E]).then_inc(s_centT, 1)
            variances(2)
            inverse_std(8, (s_std2, 2), 4)
            dve.scalar_tensor_tensor(out=shift[:, 0:4], in0=mv[:, 4:8, 0], scalar=-1.0,
                                     in1=rs[:, 4:8], op0=ALU.mult, op1=ALU.mult).then_inc(s_shift2, 1)
            centre_and_gain(1)
            residual(1)
            variances(3)

            def take(half):
                rows = slice(4 * half, 4 * half + 4)
                if half == 1:
                    cut = slice(half * 512, (half + 1) * 512)
                    dve.wait_ge(s_xfhi, half + 1)
                    dve.tensor_tensor(xf_lo[:, cut], xfT[:, cut], xf_hi[:, cut].bitcast(F32), ALU.subtract)\
                       .then_inc(s_xflo, 1)
                dve.wait_ge(s_aff, half + 1)
                dve.tensor_tensor(biased[:, rows, :],
                                  ps[:, 6 + half, 0:4 * E].rearrange("p (j e) -> p j e", j=4),
                                  bias_row[:, :].unsqueeze(1).broadcast_to([P, 4, E]), ALU.add)\
                   .then_inc(s_biased, 1)

            def find(half):
                for j in range(4 * half, 4 * half + 4):
                    chain(dve.max(top8[:, j, :], biased[:, j, :]))
                chained()
                for j in range(4 * half, 4 * half + 4):
                    chain(dve.match_replace(left[:, j, :], top8[:, j, :], biased[:, j, :], LEAST))

            expert_input()
            take(0)
            dve.wait_ge(s_biased, 1)
            find(0)
            take(1)
            dve.wait_ge(s_biased, 2)
            find(1)
            chained()
            dve.wait_ge(s_sigmoid, 1)
            chain(dve.scalar_tensor_tensor(out=gate[:, :, :], in0=left[:, :, :], scalar=LEAST,
                                           in1=gate[:, :, :], op0=ALU.is_equal, op1=ALU.mult))
            chained()
            chain(dve.tensor_reduce(w_sum[:, 0, :], gate[:, :, :], AX_X, ALU.add))
            chained()
            chain(dve.tensor_scalar(w_sum[:, 0, :], w_sum[:, 0, :], COMBINE_EPS, 1.0 / RANGE16, ALU.add, ALU.mult))
            chained()
            chain(dve.reciprocal(w_sum[:, 1, :], w_sum[:, 0, :]))
            chained()
            chain(dve.tensor_tensor(combine[:, :, :], gate[:, :, :],
                                    w_sum[:, 1, :].unsqueeze(2).broadcast_to([P, NT, E]), ALU.mult))
            chained()
            chain(dve.tensor_copy(cw16[:, :, 0, :], combine[:, :, :]))
            chained()
            dve.tensor_tensor(cw16[:, :, 1, :], combine[:, :, :], cw16[:, :, 0, :], ALU.subtract)\
               .then_inc(s_cw, 1)
            dve.wait_ge(s_cwt, 1)
            dve.tensor_copy(cwT16[:, :], ps[:, CW_BANK, :].bitcast(F16)).then_inc(s_cwT, 1)

            def weigh(f):
                dve.wait_ge(s_silu, f + 1)
                dve.wait_ge(s_cwb, f + 1)
                hv = h_all[:, bass.ds(f * T, T)].rearrange("p (a c) -> p a c", a=2)
                dve.tensor_tensor(hv, hv, ps[:, CW_BANK:CW_BANK + 2, :], ALU.mult).then_inc(s_h, 1)

            def h_low(f, u):
                dve.wait_ge(s_hhi, f + 1)
                dve.tensor_tensor(h_lo[:, u, :], h_all[:, bass.ds(f * T, T)], h_hi[:, u, :].bitcast(F32), ALU.subtract)\
                   .then_inc(s_hlo, 1)

            dve.wait_ge(s_shi, 1)
            dve.tensor_tensor(h_lo[0:FF, 1, :], hs[:, :], h_hi[0:FF, 1, :].bitcast(F32), ALU.subtract)\
               .then_inc(s_slo, 1)
            weigh(0)
            weigh(1)
            h_low(0, 0)
            with dve.Fori(0, CLOSING // 2) as i:
                for u in range(2):
                    weigh(i * 2 + (2 + u))
                    h_low(i * 2 + (1 + u), 1 - u)
            for what, f in closing_low:
                if what == "weigh":
                    weigh(f)
                elif f < LAST:
                    h_low(f, f % 2)
                else:
                    dve.wait_ge(s_hhi, f + 1)
                    dve.tensor_tensor(last_lo[:, f - LAST, :], h[:, f, :], last_hi[:, f - LAST, :].bitcast(F32),
                                      ALU.subtract).then_inc(s_hlo, 1)
            dve.wait_ge(s_last, 1)
            dve.tensor_copy(yT[:, 0:512], ps[:, Y_BANK, :]).then_inc(s_yT[0], 1)
            for half in range(2):
                dve.wait_ge(s_yt, half + 1)
                dve.tensor_tensor(y_out[:, 4 * half:4 * half + 4, :],
                                  ps[:, 2 + half, :].rearrange("p (j d) -> p j d", j=4),
                                  x1[:, 4 * half:4 * half + 4, :], ALU.add).then_inc(s_y, 1)


INPUTS = ["x", "ctx_1024", "mask_BxS2_bf1", "L0_xattn_g_x", "L0_xattn_b_x", "L0_xattn_g_l", "L0_xattn_b_l",
          "L0_xattn_Wq", "L0_xattn_Wkv", "L0_xattn_Wout", "L0_xattn_g_o", "L0_xattn_b_o",
          "L0_ffn_centroids", "L0_ffn_expert_biases", "L0_ffn_Ws_up", "L0_ffn_Ws_down", "L0_ffn_W_up",
          "L0_ffn_W_down"]


def kernel(**inputs):
    import numpy as np
    import concourse.bacc as bacc
    from concourse.bass_utils import run_bass_kernel_spmd

    nc = bacc.Bacc("TRN2", target_bir_lowering=False, num_devices=1)
    arrays, args = {}, []
    for name in INPUTS:
        a = np.ascontiguousarray(inputs[name])
        if a.dtype == np.bool_:
            a = a.view(np.uint8)
        arrays["in_" + name] = a
        args.append(nc.dram_tensor("in_" + name, a.shape, mybir.dt.from_np(a.dtype), kind="ExternalInput").ap())
    shape = inputs["x"].shape
    args.append(nc.dram_tensor("out_0", shape, F32, kind="ExternalOutput").ap())
    xattn_moe(nc, *args)
    r = run_bass_kernel_spmd(nc, [arrays], core_ids=[0])
    return r.results[0]["out_0"]
```
